# Optimizing a Trainium2 kernel written in Bass

```python
import numpy as np
import jax
import jax.numpy as jnp

def _softmax(x, axis=-1):
    return jax.nn.softmax(x, axis=axis)

def _gelu(x):
    return jax.nn.gelu(x, approximate=True)

def _silu(x):
    return jax.nn.silu(x)

def _sigmoid(x):
    return jax.nn.sigmoid(x)

def _layernorm(x, axis=-1, eps=1e-05):
    m = jnp.mean(x, axis=axis, keepdims=True)
    v = jnp.var(x, axis=axis, keepdims=True)
    return (x - m) / jnp.sqrt(v + eps)

def _scatter_add(tgt, idx, src, axis=0):
    return tgt.at[idx].add(src)

def _segment_sum(src, seg, n):
    return jax.ops.segment_sum(src, seg, n)
kernel_name = 'mk_decoder_postln_d1_seqx_r8_2612d7'

def setup_inputs(seed: int=0):
    np.random.seed(seed)
    _w = jnp.asarray

    def _rec_inputs():
        import jax
        import jax.numpy as jnp
        _rk = jax.random.key(seed)
        x = -0.0002928 + 1 * jax.random.normal(jax.random.fold_in(_rk, 1), (128, 64, 128), jnp.float32)
        _lenS = 64 - jax.random.randint(jax.random.fold_in(_rk, 7), (128,), 0, max(1, 64 // 4) + 1, jnp.int32)
        _lenS2 = 64 - jax.random.randint(jax.random.fold_in(_rk, 8), (128,), 0, max(1, 64 // 4) + 1, jnp.int32)
        _ctx_1024P = jax.random.normal(jax.random.fold_in(_rk, 11), (128, 16, 128), jnp.float32)
        _ctx_1024c = jax.random.dirichlet(jax.random.fold_in(_rk, 511), 0.3 * jnp.ones((16,), jnp.float32), (128, 64))
        _ctx_1024t = jnp.einsum('bsk,bkd->bsd', _ctx_1024c, _ctx_1024P)
        _ctx_1024t = _ctx_1024t * jax.lax.rsqrt(jnp.mean(jnp.square(_ctx_1024t)) + 1e-12) * 0.953939
        ctx_1024 = -1.39393e-06 + 0.999914 * (_ctx_1024t + 0.3 * jax.random.normal(jax.random.fold_in(_rk, 611), (128, 64, 128), jnp.float32))
        _validS = jnp.arange(64)[None, :] < _lenS[:, None]
        _validS2 = jnp.arange(64)[None, :] < _lenS2[:, None]
        _causal = jnp.tril(jnp.ones((64, 64), dtype=bool))
        mask_BxS2_ik0 = jnp.where(jnp.broadcast_to(_validS2[:, :], (128, 64)), 0, 1).astype(jnp.int32)
        return (x, ctx_1024, mask_BxS2_ik0)
    x, ctx_1024, mask_BxS2_ik0 = _rec_inputs()

    def _L0_attn_setup():
        import jax, jax.numpy as jnp
        import numpy as np
        D_MODEL, N_HEADS, D_FF = (128, 16, 512)
        SCALE = 0.1
        NUM_BITS = 8
        LEVELS = 1 << NUM_BITS
        HALF = LEVELS // 2
        MAX_EXP = 4
        EPS = 1e-05

        def pow2_weight(key, shape, max_exp=MAX_EXP):
            k1, k2 = jax.random.split(key)
            sign = jax.random.randint(k1, shape, -1, 2).astype(jnp.float32)
            e = jax.random.randint(k2, shape, max_exp, max_exp + 4).astype(jnp.float32)
            return sign * jnp.exp2(-e)

        def _layernorm(x, g, b):
            mu = jnp.mean(x, axis=-1, keepdims=True)
            var = jnp.var(x, axis=-1, keepdims=True)
            return (x - mu) * jax.lax.rsqrt(var + EPS) * g + b

        def _lookup_act(x):
            grid = (jnp.arange(LEVELS, dtype=jnp.float32) - HALF) * SCALE
            table = jax.nn.gelu(grid)
            idx = jnp.clip(jnp.round(x / SCALE).astype(jnp.int32) + HALF, 0, LEVELS - 1)
            return table[idx]

        def _linear_attention(x, wq, wk, wv, wo):
            B, S, D = x.shape
            H, Dh = (N_HEADS, D // N_HEADS)
            q = (x @ wq).reshape(B, S, H, Dh)
            k = (x @ wk).reshape(B, S, H, Dh)
            v = (x @ wv).reshape(B, S, H, Dh)
            phi_q = jax.nn.elu(q) + 1.0
            phi_k = jax.nn.elu(k) + 1.0
            kv = jnp.einsum('bshd,bshe->bhde', phi_k, v)
            z = jnp.sum(phi_k, axis=1)
            num = jnp.einsum('bshd,bhde->bshe', phi_q, kv)
            den = jnp.einsum('bshd,bhd->bsh', phi_q, z)[..., None] + 1e-06
            out = (num / den).reshape(B, S, D)
            return out @ wo
        key = jax.random.key(seed)
        ks = jax.random.split(key, 8)
        x = jax.random.normal(ks[0], (4, 256, D_MODEL), dtype=jnp.float32)
        return {'x': x, 'ln1_g': jnp.ones((D_MODEL,), jnp.float32), 'ln1_b': jnp.zeros((D_MODEL,), jnp.float32), 'wq': pow2_weight(ks[1], (D_MODEL, D_MODEL)), 'wk': pow2_weight(ks[2], (D_MODEL, D_MODEL)), 'wv': pow2_weight(ks[3], (D_MODEL, D_MODEL)), 'wo': pow2_weight(ks[4], (D_MODEL, D_MODEL)), 'ln2_g': jnp.ones((D_MODEL,), jnp.float32), 'ln2_b': jnp.zeros((D_MODEL,), jnp.float32), 'w1': pow2_weight(ks[5], (D_MODEL, D_FF)), 'w2': pow2_weight(ks[6], (D_FF, D_MODEL))}
    _L0_attn_all = _L0_attn_setup()
    _L0_attn_in = {k: v for k, v in _L0_attn_all.items() if k in ('ln1_g', 'ln1_b', 'wq', 'wk', 'wv', 'wo', 'ln2_g', 'ln2_b', 'w1', 'w2')}
    del _L0_attn_all

    def _L0_xattn_setup():
        import jax, jax.numpy as jnp
        import numpy as np
        B, S, D, H = (2, 256, 128, 16)
        DK = D // H
        SQRT_DK = DK ** 0.5
        NEG = -1000000000.0
        key = jax.random.key(seed)
        ks = jax.random.split(key, 7)
        scale = 1.0 / np.sqrt(D)
        return {'x': jax.random.normal(ks[0], (B, S, D), jnp.float32), 'encoder_output': jax.random.normal(ks[1], (B, S, D), jnp.float32), 'mask': jax.random.randint(ks[2], (B, S), 0, 2, jnp.int32), 'WQ': jax.random.normal(ks[3], (D, D), jnp.float32) * scale, 'WK': jax.random.normal(ks[4], (D, D), jnp.float32) * scale, 'WV': jax.random.normal(ks[5], (D, D), jnp.float32) * scale, 'WO': jax.random.normal(ks[6], (D, D), jnp.float32) * scale}
    _L0_xattn_all = _L0_xattn_setup()
    _L0_xattn_in = {k: v for k, v in _L0_xattn_all.items() if k in ('WQ', 'WK', 'WV', 'WO')}
    del _L0_xattn_all

    def _L0_ffn_setup():
        import jax, jax.numpy as jnp
        import numpy as np
        E = 8
        K = 2
        D = 128
        B, N = (4, 512)
        DC = 64
        key = jax.random.key(seed)
        ks = jax.random.split(key, 6)
        x = jax.random.normal(ks[0], (B, N, D), jnp.float32)
        cond = jax.random.normal(ks[1], (B, N, DC), jnp.float32)
        mask = jnp.ones((B, N), jnp.float32)
        W_shared = jax.random.normal(ks[2], (D, D), jnp.float32) * 0.02
        W_expert = jax.random.normal(ks[3], (D, D), jnp.float32) * 0.02
        W_gate = jax.random.normal(ks[4], (D, E - 1), jnp.float32) * 0.02
        bias = jnp.zeros((D,), jnp.float32)
        return dict(x=x, cond=cond, mask=mask, W_shared=W_shared, W_expert=W_expert, W_gate=W_gate, bias=bias)
    _L0_ffn_all = _L0_ffn_setup()
    _L0_ffn_in = {k: v for k, v in _L0_ffn_all.items() if k in ('cond', 'mask', 'W_shared', 'W_expert', 'W_gate', 'bias')}
    del _L0_ffn_all
    return {'x': x, 'ctx_1024': ctx_1024, 'mask_BxS2_ik0': mask_BxS2_ik0, 'L0_attn_ln1_g': _L0_attn_in['ln1_g'], 'L0_attn_ln1_b': _L0_attn_in['ln1_b'], 'L0_attn_wq': _L0_attn_in['wq'], 'L0_attn_wk': _L0_attn_in['wk'], 'L0_attn_wv': _L0_attn_in['wv'], 'L0_attn_wo': _L0_attn_in['wo'], 'L0_attn_ln2_g': _L0_attn_in['ln2_g'], 'L0_attn_ln2_b': _L0_attn_in['ln2_b'], 'L0_attn_w1': _L0_attn_in['w1'], 'L0_attn_w2': _L0_attn_in['w2'], 'L0_xattn_WQ': _L0_xattn_in['WQ'], 'L0_xattn_WK': _L0_xattn_in['WK'], 'L0_xattn_WV': _L0_xattn_in['WV'], 'L0_xattn_WO': _L0_xattn_in['WO'], 'L0_ffn_cond': _L0_ffn_in['cond'], 'L0_ffn_mask': _L0_ffn_in['mask'], 'L0_ffn_W_shared': _L0_ffn_in['W_shared'], 'L0_ffn_W_expert': _L0_ffn_in['W_expert'], 'L0_ffn_W_gate': _L0_ffn_in['W_gate'], 'L0_ffn_bias': _L0_ffn_in['bias']}

def reference(x, ctx_1024, mask_BxS2_ik0, L0_attn_ln1_g, L0_attn_ln1_b, L0_attn_wq, L0_attn_wk, L0_attn_wv, L0_attn_wo, L0_attn_ln2_g, L0_attn_ln2_b, L0_attn_w1, L0_attn_w2, L0_xattn_WQ, L0_xattn_WK, L0_xattn_WV, L0_xattn_WO, L0_ffn_cond, L0_ffn_mask, L0_ffn_W_shared, L0_ffn_W_expert, L0_ffn_W_gate, L0_ffn_bias):
    import jax
    import jax.numpy as jnp

    def _L0_attn_ref(x, ln1_g, ln1_b, wq, wk, wv, wo, ln2_g, ln2_b, w1, w2):
        import jax, jax.numpy as jnp
        import numpy as np
        D_MODEL, N_HEADS, D_FF = (128, 16, 512)
        SCALE = 0.1
        NUM_BITS = 8
        LEVELS = 1 << NUM_BITS
        HALF = LEVELS // 2
        MAX_EXP = 4
        EPS = 1e-05

        def pow2_weight(key, shape, max_exp=MAX_EXP):
            k1, k2 = jax.random.split(key)
            sign = jax.random.randint(k1, shape, -1, 2).astype(jnp.float32)
            e = jax.random.randint(k2, shape, max_exp, max_exp + 4).astype(jnp.float32)
            return sign * jnp.exp2(-e)

        def _layernorm(x, g, b):
            mu = jnp.mean(x, axis=-1, keepdims=True)
            var = jnp.var(x, axis=-1, keepdims=True)
            return (x - mu) * jax.lax.rsqrt(var + EPS) * g + b

        def _lookup_act(x):
            grid = (jnp.arange(LEVELS, dtype=jnp.float32) - HALF) * SCALE
            table = jax.nn.gelu(grid)
            idx = jnp.clip(jnp.round(x / SCALE).astype(jnp.int32) + HALF, 0, LEVELS - 1)
            return table[idx]

        def _linear_attention(x, wq, wk, wv, wo):
            B, S, D = x.shape
            H, Dh = (N_HEADS, D // N_HEADS)
            q = (x @ wq).reshape(B, S, H, Dh)
            k = (x @ wk).reshape(B, S, H, Dh)
            v = (x @ wv).reshape(B, S, H, Dh)
            phi_q = jax.nn.elu(q) + 1.0
            phi_k = jax.nn.elu(k) + 1.0
            kv = jnp.einsum('bshd,bshe->bhde', phi_k, v)
            z = jnp.sum(phi_k, axis=1)
            num = jnp.einsum('bshd,bhde->bshe', phi_q, kv)
            den = jnp.einsum('bshd,bhd->bsh', phi_q, z)[..., None] + 1e-06
            out = (num / den).reshape(B, S, D)
            return out @ wo
        x = x + _linear_attention(_layernorm(x, ln1_g, ln1_b), wq, wk, wv, wo)
        h = _layernorm(x, ln2_g, ln2_b)
        x = x + _lookup_act(h @ w1) @ w2
        return x

    def _L0_xattn_ref(x, encoder_output, mask, WQ, WK, WV, WO):
        import jax, jax.numpy as jnp
        import numpy as np
        B, S, D, H = (2, 256, 128, 16)
        DK = D // H
        SQRT_DK = DK ** 0.5
        NEG = -1000000000.0
        b, s, d = x.shape
        q = (x @ WQ).reshape(b, s, H, DK).transpose(0, 2, 1, 3)
        k = (encoder_output @ WK).reshape(b, s, H, DK).transpose(0, 2, 1, 3)
        v = (encoder_output @ WV).reshape(b, s, H, DK).transpose(0, 2, 1, 3)
        scores = jnp.einsum('bhqd,bhkd->bhqk', q, k) / SQRT_DK
        future = jnp.triu(jnp.ones((s, s), jnp.int32), 1)
        m = mask[:, None, :, None] + future[None, None, :, :]
        scores = jnp.where(m != 0, NEG, scores)
        attn = jax.nn.softmax(scores, axis=-1)
        ctx = jnp.einsum('bhqk,bhkd->bqhd', attn, v).reshape(b, s, d)
        return ctx @ WO

    def _L0_ffn_ref(x, cond, mask, W_shared, W_expert, W_gate, bias):
        import jax, jax.numpy as jnp
        import numpy as np
        E = 8
        K = 2
        D = 128
        B, N = (4, 512)
        DC = 64
        b, n, d = x.shape
        T = b * n
        xf = x.reshape(T, d)
        scores = jax.nn.softmax(xf @ W_gate, axis=-1)
        expert_weights, _ = jax.lax.top_k(scores, K)
        expert_weights = expert_weights / expert_weights.sum(-1, keepdims=True)
        expert_indices = (jnp.arange(T * K) % E).reshape(T, K)
        te = expert_indices.reshape(-1)
        w = expert_weights.reshape(-1)
        capacity = K * T // E
        order = jnp.argsort(te, stable=True)
        sorted_e = te[order]
        hist = jnp.bincount(te, length=E)
        starts = jnp.concatenate([jnp.zeros((1,), hist.dtype), jnp.cumsum(hist)[:-1]])
        pos = jnp.arange(T * K) - starts[sorted_e]
        valid = pos < capacity
        dest = jnp.where(valid, sorted_e * capacity + pos, E * capacity)
        tok = order // K
        gathered = jnp.zeros((E * capacity + 1, d), x.dtype).at[dest].set(xf[tok])
        gathered = gathered[:-1]
        y = gathered @ W_expert.T
        contrib = w[order][:, None] * y[jnp.minimum(dest, E * capacity - 1)]
        moe_out = jnp.zeros((T, d), x.dtype).at[tok].add(jnp.where(valid[:, None], contrib, 0.0))
        shared = xf @ W_shared.T
        out = (shared + moe_out + bias).reshape(b, n, d)
        return out
    x = _layernorm(x + _L0_attn_ref(x, L0_attn_ln1_g, L0_attn_ln1_b, L0_attn_wq, L0_attn_wk, L0_attn_wv, L0_attn_wo, L0_attn_ln2_g, L0_attn_ln2_b, L0_attn_w1, L0_attn_w2), axis=-1)
    x = _layernorm(x + _L0_xattn_ref(x, ctx_1024, mask_BxS2_ik0, L0_xattn_WQ, L0_xattn_WK, L0_xattn_WV, L0_xattn_WO), axis=-1)
    x = _layernorm(x + _L0_ffn_ref(x, L0_ffn_cond, L0_ffn_mask, L0_ffn_W_shared, L0_ffn_W_expert, L0_ffn_W_gate, L0_ffn_bias), axis=-1)
    return x

_drawn_inputs = setup_inputs


def setup_inputs(seed=0):
    import zlib

    import numpy as np

    out = dict(_drawn_inputs(seed))
    spreads = {'L0_attn_ln1_g': (1.0, 0.6),
     'L0_attn_ln1_b': (0.0, 0.8),
     'L0_attn_ln2_g': (1.0, 0.6),
     'L0_attn_ln2_b': (0.0, 2.0),
     'L0_ffn_bias': (0.0, 0.1)}
    factors = {'L0_attn_wq': 8.0,
     'L0_attn_wk': 8.0,
     'L0_attn_wv': 6.595,
     'L0_attn_wo': 6.545,
     'L0_ffn_W_gate': 64.0}
    for name, (base, spread) in spreads.items():
        noise = np.random.default_rng([zlib.crc32(name.encode()), seed]).standard_normal(out[name].shape)
        drawn = base * np.exp(spread * noise) if base else spread * noise
        out[name] = jnp.asarray(drawn.astype(out[name].dtype))
    for name, factor in factors.items():
        out[name] = (out[name] * factor).astype(out[name].dtype)
    return out
```

```python
from contextlib import ExitStack

import numpy as np
import concourse.bass as bass
from concourse import mybir

F32 = mybir.dt.float32
BF16 = mybir.dt.bfloat16
I32 = mybir.dt.int32
ALU = mybir.AluOpType
ACT = mybir.ActivationFunctionType
AX = mybir.AxisListType

P = 128
B, S, D = 128, 64, 128
H = 16
DH = D // H
FF = 512
NF = FF // P
NT = B * S // P
TG = 4
NG = NT // TG
GW = TG * P
HV = DH + 1
HH = H // 2
FH = D // 2
NE = 7
TOPW = 8
EPS = 1e-5
DEN_EPS = 1e-6
LEVELS = 256
HALF = LEVELS // 2
QSTEP = 0.1
ROUND = 1.5 * 2.0 ** 23
NEG = -2.0 ** 32
LOWEST = -3.0e38


def decoder_layer(nc, x, ctx, mask, ln1_g, ln1_b, wq, wk, wv, wo, ln2_g, ln2_b, w1, w2,
                  xq, xk, xv, xo, w_shared_t, w_expert_t, w_gate, bias, out):
    es = ExitStack()

    def sb(name, shape, dt=F32):
        return es.enter_context(nc.sbuf_tensor(name, shape, dt))

    def pb(name, shape, dt=F32):
        return es.enter_context(nc.psum_tensor(name, shape, dt))

    def sem(name):
        return es.enter_context(nc.semaphore(name))

    x_tiles = x.rearrange("(n p) d -> p n d", p=P)
    ctx_tiles = ctx.rearrange("(n p) d -> p n d", p=P)
    out_tiles = out.rearrange("(n p) d -> p n d", p=P)

    with es:
        X = sb("X", [P, NT, D])
        X1 = sb("X1", [P, NT, D])

        w_q = sb("w_q", [P, D])
        w_kv = sb("w_kv", [P, 2 * D])
        w_o = sb("w_o", [P, D])
        w_1 = sb("w_1", [P, FF])
        w_1s = sb("w_1s", [P, FF])
        w_2 = sb("w_2", [P, NF, D])
        w_xq = sb("w_xq", [P, D])
        w_xk = sb("w_xk", [P, D])
        w_xv = sb("w_xv", [P, D])
        w_xo = sb("w_xo", [P, D])
        w_moe = sb("w_moe", [P, 2 * D + NE])
        affine = sb("affine", [P, 4])
        bias_bc = sb("bias_bc", [P, D])
        mask_i = sb("mask_i", [P, NT], I32)
        row_scale = sb("row_scale", [P, NT])
        ident = sb("ident", [P, P])
        ident_bf = sb("ident_bf", [P, P], BF16)
        head_mask = sb("head_mask", [P, H, HV])
        half_mask = sb("half_mask", [P, HH])
        causal = sb("causal", [P, HH, S])
        causal_bf = sb("causal_bf", [P, HH * S], BF16)
        minus_half = sb("minus_half", [P, TG])
        zero_col = sb("zero_col", [P, TG])

        stats = sb("stats", [P, TG, 6])
        mv = [sb(f"mv{i}", [P, TG, 2]) for i in range(2)]
        veps = sb("veps", [P, TG])
        rstd = [sb(f"rstd{i}", [P, TG]) for i in range(2)]
        stats_b = sb("stats_b", [P, TG, 6])
        mv_b = sb("mv_b", [P, TG, 2])
        veps_b = sb("veps_b", [P, TG])
        rstd_b = sb("rstd_b", [P, TG])
        stats_c = sb("stats_c", [P, TG, 6])
        mv_c = sb("mv_c", [P, TG, 2])
        veps_c = sb("veps_c", [P, TG])
        rstd_c = sb("rstd_c", [P, TG])
        xn = [sb(f"xn{i}", [P, TG, D]) for i in range(2)]
        hT = [sb(f"hT{i}", [P, GW]) for i in range(2)]
        att = [sb(f"att{i}", [P, TG, D]) for i in range(2)]
        attT = sb("attT", [P, GW])
        den = sb("den", [P, H])
        rec = sb("rec", [P, H])
        expqk = [sb(f"expqk{i}", [P, 2, GW]) for i in range(2)]
        phi_q = [sb(f"phi_q{i}", [P, GW]) for i in range(2)]
        phi_k = [sb(f"phi_k{i}", [P, TG, D]) for i in range(2)]
        v_ext = [sb(f"v_ext{i}", [P, TG, 2, H * HV]) for i in range(2)]
        kv_m = [sb(f"kv_m{i}", [P, 2, H * HV]) for i in range(2)]
        rnd = [sb(f"rnd{i}", [P, GW]) for i in range(2)]
        lev = [sb(f"lev{i}", [P, GW], BF16) for i in range(2)]
        gel = sb("gel", [P, 2, NF, GW])
        k_exp = X1[:, :, :].rearrange("p n d -> p (n d)").rearrange(
            "p (q g t h k) -> p q g t h k", q=2, g=2, t=TG, h=HH)
        big = gel[:, :, :, :].rearrange("p q f n -> p (q f n)")
        s_sub = [big[:, 1024 * i:1024 * (i + 1)] for i in range(2)]
        pT = [big[:, 2048 + 1024 * i:2048 + 1024 * (i + 1)] for i in range(2)]
        ctx_in = [sb(f"ctx_in{i}", [P, TG, D]) for i in range(2)]
        y_in = xn
        yT = hT[0]
        cT = hT[1]
        q_bd = [sb(f"q_bd{i}", [P, 2, TG, P]) for i in range(2)]
        k_sb = sb("k_sb", [P, 2, TG, S])
        v2 = [sb(f"v2{i}", [P, 2 * TG, HH, 2, HV]) for i in range(2)]
        neg_max = [sb(f"neg_max{i}", [P, H]) for i in range(2)]
        y2 = sb("y2", [P, TG, D])
        y2b = sb("y2b", [P, TG, D])
        y2T = sb("y2T", [P, GW])
        moe_s = [sb(f"moe_s{i}", [P, TG, D]) for i in range(2)]
        moe_e = [sb(f"moe_e{i}", [P, TG, D + TOPW]) for i in range(2)]
        top = sb("top", [P, TG, TOPW])
        top_e = sb("top_e", [P, TG, TOPW])
        top_z = sb("top_z", [P, TG])
        top_p = sb("top_p", [P, TG, 2])
        top_s = sb("top_s", [P, TG])
        top_w = sb("top_w", [P, TG, 2])
        top_sum = sb("top_sum", [P, TG])

        pair = [pb(f"pair{i}", [P, 2, 512]) for i in range(4)]

        def bank(i):
            return pair[i // 2][:, i % 2, :]

        w_loaded = sem("w_loaded")
        x_loaded = [sem(f"x_loaded{i}") for i in range(2)]
        ctx_loaded = [sem(f"ctx_loaded{i}") for i in range(2)]
        out_stored = sem("out_stored")
        const_step, const_ready, const_dve = sem("const_step"), sem("const_ready"), sem("const_dve")

        passed = {e.engine: sem(f"passed_{n}") for n, e in
                  (("act", nc.scalar), ("dve", nc.vector), ("pool", nc.gpsimd))}

        class Norm:
            def __init__(self, name):
                self.stats, self.mv, self.eps, self.rstd, self.done = (
                    sem(f"{name}_{n}") for n in ("stats", "mv", "eps", "rstd", "done"))

        ln1, ln2, ln_a, ln_b, ln_c = (Norm(n) for n in ("ln1", "ln2", "ln_a", "ln_b", "ln_c"))
        xn_xposed, hT_ready = sem("xn_xposed"), sem("hT_ready")
        q_done, kv_done = sem("q_done"), sem("kv_done")
        expq_ready, expk_ready, v_ready = sem("expq_ready"), sem("expk_ready"), sem("v_ready")
        minq_ready, mink_ready = sem("minq_ready"), sem("mink_ready")
        phiq_ready, phik_ready = sem("phiq_ready"), sem("phik_ready")
        kvsum_done, kvm_ready, num_done = sem("kvsum_done"), sem("kvm_ready"), sem("num_done")
        den_ready, rec_ready, att_ready = sem("den_ready"), sem("rec_ready"), sem("att_ready")
        att_xposed, attT_ready, proj_done = sem("att_xposed"), sem("attT_ready"), sem("proj_done")
        x1_ready, xs_ready = sem("x1_ready"), sem("xs_ready")
        h2_xposed, h2T_ready = sem("h2_xposed"), sem("h2T_ready")
        up_done, rnd_ready, lev_ready, gel_ready = (sem(n) for n in
            ("up_done", "rnd_ready", "lev_ready", "gel_ready"))
        down_done, ysum_ready = sem("down_done"), sem("ysum_ready")
        y_copied, y_xposed, c_xposed, yT_ready, cT_ready = (sem(n) for n in
            ("y_copied", "y_xposed", "c_xposed", "yT_ready", "cT_ready"))
        xq_done, xk_done, qbd_ready, ksb_ready, kexp_ready = (sem(n) for n in
            ("xq_done", "xk_done", "qbd_ready", "ksb_ready", "kexp_ready"))
        xv_done, v2_ready = sem("xv_done"), sem("v2_ready")
        s_done, max_ready, sub_ready, exp_ready = (sem(n) for n in
            ("s_done", "max_ready", "sub_ready", "exp_ready"))
        p_xposed, pT_ready, pv_done = sem("p_xposed"), sem("pT_ready"), sem("pv_done")
        xrec_ready, xatt_ready, xatt_xposed, xattT_ready = (sem(n) for n in
            ("xrec_ready", "xatt_ready", "xatt_xposed", "xattT_ready"))
        xproj_done, y1_ready, y2_xposed, y2T_ready, y2b_ready = (sem(n) for n in
            ("xproj_done", "y1_ready", "y2_xposed", "y2T_ready", "y2b_ready"))
        moe_done, moe_ready = sem("moe_done"), sem("moe_ready")
        top_ready, topd_ready, tope_ready, gate_step, osum_ready = (sem(n) for n in
            ("top_ready", "topd_ready", "tope_ready", "gate_step", "osum_ready"))

        block = es.enter_context(nc.Block())

        def after(eng, semaphore, count):
            if not isinstance(count, int) or count > 0:
                eng.wait_ge(semaphore, count)

        def apart(eng):
            eng.sem_inc(passed[eng.engine])

        def pipeline(eng, step, last=NG):
            for s in (-1, 0, 1):
                step(s, s % 2)
            with eng.Fori(1, NG // 2 - 1) as i:
                step(i * 2, 0)
                step(i * 2 + 1, 1)
            for s in range(NG - 2, last + 1):
                step(s, s % 2)

        def exists(g):
            return not isinstance(g, int) or 0 <= g < NG

        def tiles(g):
            return bass.ds(g * TG, TG)

        def ln_statistics(dve, ln, g, rows, stats, mv):
            apart(dve)
            for t in range(TG):
                last = nc.vector.bn_stats(stats[:, t, :], rows(t))
            last.then_inc(ln.stats, 1)
            dve.wait_ge(ln.stats, g + 1)
            apart(dve)
            for t in range(TG):
                last = nc.vector.bn_aggr(mv[:, t, :], stats[:, t, :])
            last.then_inc(ln.mv, 1)

        def ln_deviation(pool, ln, g, mv, veps, rstd):
            pool.wait_ge(ln.mv, g + 1)
            apart(pool)
            nc.gpsimd.tensor_scalar(veps[:, :], mv[:, :, 1], EPS, None, ALU.add).then_inc(ln.eps, 1)
            pool.wait_ge(ln.eps, g + 1)
            nc.gpsimd.tensor_tensor(rstd[:, :], veps[:, :], minus_half[:, :], ALU.pow)\
                .then_inc(ln.rstd, 1)

        def ln_rows(dve, ln, g, rows, outs, mv, rstd):
            dve.wait_ge(ln.rstd, g + 1)
            for t in range(TG):
                last = nc.vector.tensor_scalar(outs(t), rows(t), mv[:, t, 0:1], rstd[:, t:t + 1],
                                               ALU.subtract, ALU.mult)
            last.then_inc(ln.done, 1)

        weights = [(affine[:, 0:1], ln1_g), (affine[:, 1:2], ln1_b), (w_q[:, :], wq),
                   (w_kv[:, 0:D], wk), (w_kv[:, D:2 * D], wv), (w_o[:, :], wo),
                   (affine[:, 2:3], ln2_g), (affine[:, 3:4], ln2_b), (w_1[:, :], w1),
                   (w_2[:, :, :], w2.rearrange("(f p) d -> p f d", p=P)),
                   (w_xq[:, :], xq), (w_xk[:, :], xk), (w_xv[:, :], xv), (w_xo[:, :], xo),
                   (w_moe[:, 0:D], w_shared_t), (w_moe[:, D:2 * D], w_expert_t),
                   (w_moe[:, 2 * D:], w_gate), (bias_bc[:, :], bias.partition_broadcast(P)),
                   (mask_i[:, :], mask)]
        ALL_WEIGHTS = 16 * len(weights)

        @block.sync
        def _(sp):
            def load_x(g, p):
                sp.dma_start(X[:, tiles(g), :], x_tiles[:, tiles(g), :]).then_inc(x_loaded[p], 16)

            def load_ctx(g, p):
                sp.dma_start(ctx_in[p][:, :, :], ctx_tiles[:, tiles(g), :])\
                    .then_inc(ctx_loaded[p], 16)

            def store(g):
                sp.wait_ge(ln_c.done, g + 1)
                sp.dma_start(out_tiles[:, tiles(g), :], X[:, tiles(g), :]).then_inc(out_stored, 16)

            load_x(0, 0)
            load_x(1, 1)
            for dst, src in weights:
                sp.dma_start(dst, src).then_inc(w_loaded, 16)
            with sp.Fori(1, NG // 2) as i:
                for p in range(2):
                    sp.wait_ge(x_loaded[p], i * 16)
                    load_x(i * 2 + p, p)
            load_ctx(0, 0)
            load_ctx(1, 1)

            def turn(g, p):
                sp.wait_ge(c_xposed, g - 1)
                load_ctx(g, p)

            for g in range(2, 6):
                turn(g, g % 2)
            with sp.Fori(3, NG // 2) as i:
                for p in range(2):
                    turn(i * 2 + p, p)
                    store(i * 2 + (p - 6))
            for g in range(NG - 6, NG):
                store(g)
            sp.wait_ge(out_stored, 16 * NG)

        @block.gpsimd
        def _(pool):
            count = 0

            def const(op):
                nonlocal count
                count += 1
                op.then_inc(const_step, 1)
                pool.wait_ge(const_step, count)

            select = nc.gpsimd.affine_select
            nc.gpsimd.memset(minus_half[:, :], -0.5)
            const(nc.gpsimd.memset(ident[:, :], 0.0))
            const(select(out=ident[:, :], in_=ident[:, :], compare_op=ALU.not_equal, fill=1.0,
                         base=0, pattern=[[-1, P]], channel_multiplier=1))
            const(nc.gpsimd.memset(head_mask[:, :, :], 1.0))
            const(select(out=head_mask[:, :, :], in_=head_mask[:, :, :], compare_op=ALU.is_ge,
                         fill=0.0, base=0, pattern=[[-DH, H], [0, HV]], channel_multiplier=1))
            const(select(out=head_mask[:, :, :], in_=head_mask[:, :, :], compare_op=ALU.is_ge,
                         fill=0.0, base=DH - 1, pattern=[[DH, H], [0, HV]], channel_multiplier=-1))
            for i in range(2):
                const(nc.gpsimd.memset(v_ext[i][:, :, :, :], 0.0))
                for b in range(2):
                    half = v_ext[i][b * S:(b + 1) * S, :, b, :].rearrange("p t (h e) -> p t h e", e=HV)
                    const(nc.gpsimd.memset(half[:, :, :, DH:HV], 1.0))
            nc.gpsimd.memset(half_mask[:, :], 1.0).then_inc(const_ready, 1)
            const(nc.gpsimd.memset(causal[:, :, :], 0.0))
            for b in range(2):
                m = half_mask[b * S:(b + 1) * S, :]
                const(select(out=m, in_=m, compare_op=ALU.is_ge, fill=0.0, base=0,
                             pattern=[[-DH, HH]], channel_multiplier=1))
                const(select(out=m, in_=m, compare_op=ALU.is_ge, fill=0.0, base=DH - 1,
                             pattern=[[DH, HH]], channel_multiplier=-1))
                c = causal[b * S:(b + 1) * S, :, :]
                const(select(out=c, in_=c, compare_op=ALU.is_ge, fill=NEG, base=0,
                             pattern=[[0, HH], [-1, S]], channel_multiplier=1))
            for i in range(2):
                const(nc.gpsimd.memset(q_bd[i][:, :, :, :], 0.0))
                const(nc.gpsimd.memset(v2[i][:, :, :, :, :], 0.0))
                for h in range(2):
                    const(nc.gpsimd.memset(v2[i][h * S:(h + 1) * S, :, :, h, DH:HV], 1.0))
                const(nc.gpsimd.memset(moe_e[i][:, :, D + NE:], LOWEST))
            nc.gpsimd.memset(zero_col[:, :], 0.0).then_inc(const_ready, 1)

            def phase1(s, p):
                g, q = s + 1, 1 - p
                if exists(g):
                    ln_deviation(pool, ln1, g, mv[q], veps, rstd[q])
                    pool.wait_ge(expq_ready, g + 1)
                    apart(pool)
                    nc.gpsimd.tensor_scalar(expqk[q][:, 0, :], expqk[q][:, 0, :], 1.0, None, ALU.min)\
                        .then_inc(minq_ready, 1)
                    pool.wait_ge(expk_ready, g + 1)
                    apart(pool)
                    nc.gpsimd.tensor_scalar(expqk[q][:, 1, :], expqk[q][:, 1, :], 1.0, None, ALU.min)\
                        .then_inc(mink_ready, 1)
                g = s - 1
                if exists(g):
                    pool.wait_ge(x1_ready, g + 1)
                    nc.gpsimd.tensor_tensor(X[:, tiles(g), :], X[:, tiles(g), :],
                                            X1[:, tiles(g), :], ALU.add).then_inc(xs_ready, 1)

            def phase2(s, p):
                if exists(s + 1):
                    ln_deviation(pool, ln2, s + 1, mv[1 - p], veps, rstd[1 - p])
                if exists(s - 1):
                    ln_deviation(pool, ln_a, s - 1, mv_b, veps_b, rstd_b)

            def copy_y(g, p):
                pool.wait_ge(ln_a.done, g + 1)
                pool.wait_ge(h2_xposed, NG)
                after(pool, y_xposed, g - 1)
                apart(pool)
                nc.gpsimd.tensor_copy(y_in[p][:, :, :], X[:, tiles(g), :]).then_inc(y_copied, 1)

            def phase3(s, p):
                if exists(s + 2):
                    copy_y(s + 2, p)
                if exists(s - 1):
                    ln_deviation(pool, ln_b, s - 1, mv_b, veps_b, rstd_b)
                if exists(s - 2):
                    ln_deviation(pool, ln_c, s - 2, mv_c, veps_c, rstd_c)
                for half in range(2):
                    g, q = s + 1, 1 - p
                    if exists(g):
                        pool.wait_ge(ksb_ready, g + 1)
                        after(pool, s_done, g * TG - TG)
                        apart(pool)
                        for h in range(HH):
                            last = nc.gpsimd.tensor_scalar(
                                k_exp[:, q, half, :, h, :], k_sb[:, half, :, :],
                                half_mask[:, h:h + 1], 0.0, ALU.mult, ALU.add)
                        if half == 1:
                            last.then_inc(kexp_ready, 1)
                    g = s - 1
                    if exists(g) and half == 0:
                        pool.wait_ge(ln_b.done, g + 1)
                        after(pool, moe_ready, g * TG)
                        for t in range(TG):
                            last = nc.gpsimd.tensor_tensor(y2b[:, t, :], y2[:, t, :], bias_bc[:, :],
                                                           ALU.add)
                        last.then_inc(y2b_ready, 1)

            pipeline(pool, phase1)
            pipeline(pool, phase2)
            copy_y(0, 0)
            pool.wait_ge(w_loaded, ALL_WEIGHTS)
            pool.wait_ge(ln2.done, NG)
            pipeline(pool, phase3, last=NG + 1)

        @block.scalar
        def _(act):
            nc.scalar.preload_act_table(ACT.Exp)
            act.wait_ge(w_loaded, ALL_WEIGHTS)

            def phase1(s, p):
                g, q = s + 1, 1 - p
                if exists(g):
                    act.wait_ge(xn_xposed, g + 1)
                    after(act, kv_done, g - 1)
                    nc.scalar.activation(hT[q][:, :], bank(0), ACT.Identity, bias=affine[:, 1:2],
                                         scale=affine[:, 0:1]).then_inc(hT_ready, 1)
                g = s - 1
                if exists(g):
                    act.wait_ge(att_xposed, g + 1)
                    after(act, proj_done, g)
                    nc.scalar.activation(attT[:, :], bank(4), ACT.Copy).then_inc(attT_ready, 1)
                g = s + 1
                if exists(g):
                    act.wait_ge(q_done, g + 1)
                    after(act, phik_ready, g - 1)
                    nc.scalar.activation(expqk[q][:, 0, :], bank(1), ACT.Exp).then_inc(expq_ready, 1)
                    act.wait_ge(kv_done, g + 1)
                    kv = pair[3][:, :, :].rearrange("p a (t c) -> p (a t) c", c=2 * D)
                    nc.scalar.activation(expqk[q][:, 1, :].rearrange("p (t d) -> p t d", d=D),
                                         kv[:, :, 0:D], ACT.Exp).then_inc(expk_ready, 1)
                    after(act, kvsum_done, g * TG - TG)
                    for b in range(2):
                        rows = slice(b * S, (b + 1) * S)
                        last = nc.scalar.activation(
                            v_ext[q][rows, :, b, :].rearrange("p t (h e) -> p t h e", e=HV)[:, :, :, 0:DH],
                            kv[rows, :, D:2 * D].rearrange("p t (h e) -> p t h e", e=DH), ACT.Copy)
                    last.then_inc(v_ready, 1)

            def phase2(s, p):
                g, q = s + 1, 1 - p
                if exists(g):
                    act.wait_ge(h2_xposed, g + 1)
                    after(act, up_done, g * NF - NF)
                    nc.scalar.activation(hT[q][:, :], bank(0), ACT.Identity, bias=affine[:, 3:4],
                                         scale=affine[:, 2:3]).then_inc(h2T_ready, 1)
                if exists(s):
                    after(act, down_done, s - 1)
                    for f in range(NF):
                        act.wait_ge(lev_ready, s * NF + f + 1)
                        nc.scalar.activation(gel[:, p, f, :], lev[f % 2][:, :], ACT.Gelu_apprx_tanh,
                                             scale=QSTEP).then_inc(gel_ready, 1)

            def probabilities(n, par):
                for half in range(2):
                    act.wait_ge(sub_ready, n * 2 + half + 1)
                    apart(act)
                    part = s_sub[par][:, 512 * half:512 * (half + 1)]
                    nc.scalar.activation(part, part, ACT.Exp, scale=row_scale[:, bass.ds(n, 1)])\
                        .then_inc(exp_ready, 1)

            def copy_pT(n, par):
                act.wait_ge(p_xposed, n + 1)
                after(act, pv_done, n - 1)
                nc.scalar.activation(pT[par], pair[par][:, :, :].rearrange("p a c -> p (a c)"),
                                     ACT.Copy).then_inc(pT_ready, 1)

            def phase3(s, p):
                nxt, prev, q = s + 1, s - 1, 1 - p
                for t in range(TG):
                    if t == 0 and exists(nxt):
                        act.wait_ge(y_xposed, nxt + 1)
                        after(act, xq_done, nxt)
                        nc.scalar.activation(yT[:, :], bank(4), ACT.Copy).then_inc(yT_ready, 1)
                        act.wait_ge(c_xposed, nxt + 1)
                        after(act, xv_done, nxt)
                        nc.scalar.activation(cT[:, :], bank(5), ACT.Copy).then_inc(cT_ready, 1)
                    if t == 2 and exists(nxt):
                        after(act, pv_done, nxt * TG - TG)
                        act.wait_ge(xv_done, nxt + 1)
                        for h in range(2):
                            rows = slice(h * S, (h + 1) * S)
                            last = nc.scalar.activation(
                                v2[q][rows, :, :, h, 0:DH],
                                bank(4)[rows, :].rearrange("p (b i e) -> p b i e", i=HH, e=DH),
                                ACT.Copy)
                        last.then_inc(v2_ready, 1)
                    if exists(s):
                        copy_pT(s * TG + t, t % 2)
                    if t == 0 and exists(prev):
                        act.wait_ge(xatt_xposed, prev + 1)
                        after(act, xproj_done, prev)
                        nc.scalar.activation(attT[:, :], bank(6), ACT.Copy).then_inc(xattT_ready, 1)
                    if t == 1 and exists(nxt):
                        act.wait_ge(xq_done, nxt + 1)
                        after(act, s_done, nxt * TG - TG)
                        for b in range(2):
                            rows = slice(b * S, (b + 1) * S)
                            last = nc.scalar.activation(
                                q_bd[q][rows, :, :, rows].rearrange("p g t k -> p (g t) k"),
                                bank(4)[rows, :].rearrange("p (n k) -> p n k", k=S), ACT.Copy)
                        last.then_inc(qbd_ready, 1)
                        act.wait_ge(xk_done, nxt + 1)
                        after(act, kexp_ready, nxt)
                        nc.scalar.activation(k_sb[:, :, :, :].rearrange("p g t k -> p (g t k)"),
                                             bank(5), ACT.Copy).then_inc(ksb_ready, 1)
                    if t == 2 and exists(prev):
                        act.wait_ge(y2_xposed, prev + 1)
                        after(act, moe_done, prev * TG)
                        nc.scalar.activation(y2T[:, :], bank(6), ACT.Copy).then_inc(y2T_ready, 1)
                    if exists(s) if t < TG - 1 else exists(nxt):
                        probabilities(s * TG + t + 1, (t + 1) % 2)
                    if t == 0 and exists(s - 2):
                        act.wait_ge(topd_ready, s - 1)
                        nc.scalar.activation(top_e[:, :, :], top[:, :, :], ACT.Exp)\
                            .then_inc(tope_ready, 1)

            pipeline(act, phase1)
            nc.scalar.preload_act_table(ACT.Gelu_apprx_tanh)
            pipeline(act, phase2)
            nc.scalar.preload_act_table(ACT.Exp)
            act.wait_ge(const_dve, 4)
            act.wait_ge(const_ready, 2)
            pipeline(act, phase3, last=NG + 1)

        @block.vector
        def _(dve):
            dve.wait_ge(w_loaded, ALL_WEIGHTS)
            nc.vector.tensor_scalar(w_1s[:, :], w_1[:, :], 1.0 / QSTEP, None, ALU.mult)\
                .then_inc(const_dve, 1)
            nc.vector.tensor_scalar(row_scale[:, :], mask_i[:, :], 0.0, float(DH) ** -0.5,
                                    ALU.is_equal, ALU.mult).then_inc(const_dve, 1)
            dve.wait_ge(const_ready, 2)
            nc.vector.tensor_copy(ident_bf[:, :], ident[:, :]).then_inc(const_dve, 1)
            nc.vector.tensor_copy(causal_bf[:, :], causal[:, :, :].rearrange("p h k -> p (h k)"))\
                .then_inc(const_dve, 1)

            def kv_sum(n, t):
                dve.wait_ge(kvsum_done, n + 1)
                after(dve, num_done, n - 1)
                nc.vector.tensor_tensor(
                    kv_m[t % 2][:, :, :],
                    bank(2 + t % 2)[:, 0:2 * H * HV].rearrange("p (b c) -> p b c", b=2),
                    head_mask[:, :, :].rearrange("p h e -> p (h e)").unsqueeze(1)
                    .broadcast_to([P, 2, H * HV]), ALU.mult).then_inc(kvm_ready, 1)

            def divide(n, src, dst, first_wait, den_eps, rec_sem, done):
                sums = src[:, :, DH]
                if den_eps:
                    nc.vector.tensor_scalar(den[:, :], sums, DEN_EPS, None, ALU.add)\
                        .then_inc(den_ready, 1)
                    dve.wait_ge(den_ready, n + 1)
                    sums = den[:, :]
                nc.vector.reciprocal(rec[:, :], sums).then_inc(rec_sem, 1)
                dve.wait_ge(rec_sem, n + 1)
                nc.vector.tensor_tensor(dst, src[:, :, 0:DH],
                                        rec[:, :].unsqueeze(2).broadcast_to([P, H, DH]),
                                        ALU.mult).then_inc(done, 1)

            def attend(s, p, t):
                n = s * TG + t
                dve.wait_ge(num_done, n + 1)
                if t == 0:
                    after(dve, att_xposed, s - 1)
                src = bank(2 + t % 2)[:, 2 * H * HV:3 * H * HV].rearrange("p (h e) -> p h e", e=HV)
                divide(n, src, att[p][:, t, :].rearrange("p (h e) -> p h e", e=DH), None, True,
                       rec_ready, att_ready)

            def phase1(s, p):
                g, q = s + 1, 1 - p
                if exists(g):
                    dve.wait_ge(x_loaded[q], (g - q) * 8 + 16)
                    ln_statistics(dve, ln1, g, lambda t: X[:, g * TG + t, :], stats, mv[q])
                if exists(s):
                    kv_sum(s * TG, 0)
                    kv_sum(s * TG + 1, 1)
                if exists(g):
                    after(dve, xn_xposed, g - 1)
                    ln_rows(dve, ln1, g, lambda t: X[:, g * TG + t, :], lambda t: xn[q][:, t, :],
                            mv[q], rstd[q])
                if exists(s):
                    attend(s, p, 0)
                    kv_sum(s * TG + 2, 2)
                    attend(s, p, 1)
                    kv_sum(s * TG + 3, 3)
                if exists(s - 1):
                    r = s - 1
                    dve.wait_ge(proj_done, r + 1)
                    nc.vector.tensor_tensor(X1[:, tiles(r), :], X[:, tiles(r), :],
                                            bank(5).rearrange("p (t d) -> p t d", d=D), ALU.add)\
                        .then_inc(x1_ready, 1)
                if exists(g):
                    dve.wait_ge(minq_ready, g + 1)
                    after(dve, num_done, g * TG - TG)
                    nc.vector.scalar_tensor_tensor(phi_q[q][:, :], bank(1), 1.0, expqk[q][:, 0, :],
                                                   ALU.add, ALU.max).then_inc(phiq_ready, 1)
                    dve.wait_ge(mink_ready, g + 1)
                    dve.wait_ge(v_ready, g + 1)
                    kv = pair[3][:, :, :].rearrange("p a (t c) -> p (a t) c", c=2 * D)
                    nc.vector.scalar_tensor_tensor(
                        phi_k[q][:, :, :], kv[:, :, 0:D], 1.0,
                        expqk[q][:, 1, :].rearrange("p (t d) -> p t d", d=D), ALU.add, ALU.max)\
                        .then_inc(phik_ready, 1)
                if exists(s):
                    attend(s, p, 2)
                    attend(s, p, 3)

            def quantise(k, f):
                dve.wait_ge(up_done, k + 1)
                nc.vector.tensor_scalar(rnd[f % 2][:, :], bank(2 + f), ROUND, ROUND + HALF - 1,
                                        ALU.add, ALU.min).then_inc(rnd_ready, 1)
                dve.wait_ge(rnd_ready, k + 1)
                after(dve, gel_ready, k - 1)
                nc.vector.tensor_scalar(lev[f % 2][:, :], rnd[f % 2][:, :], ROUND - HALF, ROUND,
                                        ALU.max, ALU.subtract).then_inc(lev_ready, 1)

            def phase2(s, p):
                g, q, r = s + 1, 1 - p, s - 1
                if exists(g):
                    dve.wait_ge(x1_ready, g + 1)
                    ln_statistics(dve, ln2, g, lambda t: X1[:, g * TG + t, :], stats, mv[q])
                if exists(s):
                    quantise(s * NF, 0)
                    quantise(s * NF + 1, 1)
                if exists(g):
                    after(dve, h2_xposed, g - 1)
                    ln_rows(dve, ln2, g, lambda t: X1[:, g * TG + t, :], lambda t: xn[q][:, t, :],
                            mv[q], rstd[q])
                if exists(s - 2):
                    o = s - 2
                    ln_rows(dve, ln_a, o, lambda t: X[:, o * TG + t, :],
                            lambda t: X[:, o * TG + t, :], mv_b, rstd_b)
                if exists(s):
                    quantise(s * NF + 2, 2)
                    quantise(s * NF + 3, 3)
                if exists(r):
                    dve.wait_ge(down_done, r + 1)
                    dve.wait_ge(xs_ready, r + 1)
                    nc.vector.tensor_tensor(X[:, tiles(r), :], X[:, tiles(r), :],
                                            bank(6 + q).rearrange("p (t d) -> p t d", d=D), ALU.add)\
                        .then_inc(ysum_ready, 1)
                    dve.wait_ge(ysum_ready, r + 1)
                    ln_statistics(dve, ln_a, r, lambda t: X[:, r * TG + t, :], stats_b, mv_b)

            def shift(n, par):
                dve.wait_ge(s_done, n + 1)
                scores = pair[par][:, :, :].rearrange("p a (h k) -> p (a h) k", k=S)
                nc.vector.tensor_reduce(neg_max[par][:, :], scores, AX.X, ALU.max, negate=True)\
                    .then_inc(max_ready, 1)
                dve.wait_ge(max_ready, n + 1)
                after(dve, p_xposed, n - 1)
                for half in range(2):
                    heads = slice(HH * half, HH * (half + 1))
                    nc.vector.tensor_tensor(
                        s_sub[par][:, 512 * half:512 * (half + 1)].rearrange("p (h k) -> p h k", k=S),
                        scores[:, heads, :],
                        neg_max[par][:, heads].unsqueeze(2).broadcast_to([P, HH, S]),
                        ALU.add).then_inc(sub_ready, 1)

            def gate_top(g, p):
                apart(dve)
                for t in range(TG):
                    last = nc.vector.max(top[:, t, :], moe_e[p][:, t, D:])
                last.then_inc(top_ready, 1)
                dve.wait_ge(top_ready, g * 2 + 1)
                nc.vector.tensor_copy(top_z[:, :], top[:, :, 0]).then_inc(top_ready, 1)
                dve.wait_ge(top_ready, g * 2 + 2)
                nc.vector.tensor_tensor(top[:, :, :], top[:, :, :],
                                        top_z[:, :].unsqueeze(2).broadcast_to([P, TG, TOPW]),
                                        ALU.subtract).then_inc(topd_ready, 1)

            def mixture(g, p):
                dve.wait_ge(tope_ready, g + 1)
                step = 0

                def chain(op):
                    nonlocal step
                    step += 1
                    op.then_inc(gate_step, 1)
                    dve.wait_ge(gate_step, g * 7 + step)

                chain(nc.vector.tensor_reduce(top_z[:, :], top_e[:, :, :], AX.X, ALU.add))
                chain(nc.vector.reciprocal(top_s[:, :], top_z[:, :]))
                chain(nc.vector.tensor_tensor(top_p[:, :, :], top_e[:, :, 0:2],
                                              top_s[:, :].unsqueeze(2).broadcast_to([P, TG, 2]),
                                              ALU.mult))
                chain(nc.vector.tensor_reduce(top_z[:, :], top_p[:, :, :], AX.X, ALU.add))
                chain(nc.vector.reciprocal(top_s[:, :], top_z[:, :]))
                chain(nc.vector.tensor_tensor(top_w[:, :, :], top_p[:, :, :],
                                              top_s[:, :].unsqueeze(2).broadcast_to([P, TG, 2]),
                                              ALU.mult))
                chain(nc.vector.tensor_reduce(top_sum[:, :], top_w[:, :, :], AX.X, ALU.add))
                for t in range(TG):
                    last = nc.vector.scalar_tensor_tensor(
                        moe_s[p][:, t, :], moe_e[p][:, t, 0:D], top_sum[:, t:t + 1],
                        moe_s[p][:, t, :], ALU.mult, ALU.add)
                last.then_inc(osum_ready, 1)
                dve.wait_ge(osum_ready, g + 1)
                ln_statistics(dve, ln_c, g, lambda t: moe_s[p][:, t, :], stats_c, mv_c)

            def collect(n, t, p):
                dve.wait_ge(moe_done, n + 1)
                src = bank([4, 5, 6, 4][t])
                nc.vector.tensor_tensor(moe_s[p][:, t, :], src[:, 0:D], y2b[:, t, :], ALU.add)
                nc.vector.tensor_copy(moe_e[p][:, t, 0:D + NE], src[:, D:2 * D + NE])\
                    .then_inc(moe_ready, 1)

            def phase3(s, p):
                prev, old, q = s - 1, s - 2, 1 - p
                for t in range(TG):
                    if exists(s) if t < TG - 1 else exists(s + 1):
                        shift(s * TG + t + 1, (t + 1) % 2)
                    if t == 0 and exists(old):
                        dve.wait_ge(moe_ready, s * TG - TG)
                        gate_top(old, p)
                    if t == 1 and exists(prev):
                        dve.wait_ge(xproj_done, prev + 1)
                        nc.vector.tensor_tensor(X[:, tiles(prev), :], X[:, tiles(prev), :],
                                                bank(6).rearrange("p (t d) -> p t d", d=D), ALU.add)\
                            .then_inc(y1_ready, 1)
                        dve.wait_ge(y1_ready, prev + 1)
                        ln_statistics(dve, ln_b, prev, lambda t: X[:, prev * TG + t, :],
                                      stats_b, mv_b)
                    if t == 1 and exists(old):
                        mixture(old, p)
                    if t == 2 and exists(prev):
                        after(dve, y2_xposed, prev)
                        after(dve, y2b_ready, prev)
                        ln_rows(dve, ln_b, prev, lambda t: X[:, prev * TG + t, :],
                                lambda t: y2[:, t, :], mv_b, rstd_b)
                    if t == 2 and exists(old):
                        ln_rows(dve, ln_c, old, lambda t: moe_s[p][:, t, :],
                                lambda t: X[:, old * TG + t, :], mv_c, rstd_c)
                    if t == 3 and exists(prev):
                        dve.wait_ge(y2b_ready, prev + 1)
                        for u in range(TG):
                            collect(prev * TG + u, u, q)
                    if exists(s):
                        n = s * TG + t
                        dve.wait_ge(pv_done, n + 1)
                        if t == 0:
                            after(dve, xatt_xposed, s - 1)
                        divide(n, bank(7)[:, 0:H * HV].rearrange("p (h e) -> p h e", e=HV),
                               att[p][:, t, :].rearrange("p (h e) -> p h e", e=DH), None, False,
                               xrec_ready, xatt_ready)

            pipeline(dve, phase1)
            pipeline(dve, phase2, last=NG + 1)
            pipeline(dve, phase3, last=NG + 1)

        @block.tensor
        def _(pe):
            pe.wait_ge(w_loaded, ALL_WEIGHTS)
            pe.wait_ge(const_ready, 1)

            def transposes(src, dst, done):
                for t in range(TG):
                    last = nc.tensor.transpose(dst[:, P * t:P * (t + 1)], src[:, t, :], ident[:, :])
                last.then_inc(done, 1)

            def kv_products(s, p, t):
                n = s * TG + t
                if t == 0:
                    pe.wait_ge(phik_ready, s + 1)
                    pe.wait_ge(v_ready, s + 1)
                after(pe, att_ready, n - 1)
                nc.tensor.matmul(bank(2 + t % 2)[:, 0:2 * H * HV], phi_k[p][:, t, :],
                                 v_ext[p][:, t, :, :].rearrange("p b c -> p (b c)"),
                                 start=True, stop=True).then_inc(kvsum_done, 1)

            def numerators(s, p, t):
                pe.wait_ge(kvm_ready, s * TG + t + 1)
                for b in range(2):
                    last = nc.tensor.matmul(
                        bank(2 + t % 2)[b * S:(b + 1) * S, 2 * H * HV:3 * H * HV],
                        phi_q[p][:, P * t + b * S:P * t + (b + 1) * S], kv_m[t % 2][:, b, :],
                        start=True, stop=True)
                last.then_inc(num_done, 1)

            def phase1(s, p):
                g, q, r = s + 1, 1 - p, s - 1
                if exists(s):
                    kv_products(s, p, 0)
                    kv_products(s, p, 1)
                if exists(g):
                    pe.wait_ge(ln1.done, g + 1)
                    after(pe, hT_ready, g)
                    transposes(xn[q], bank(0), xn_xposed)
                if exists(s):
                    numerators(s, p, 0)
                    kv_products(s, p, 2)
                if exists(r):
                    pe.wait_ge(att_ready, r * TG + TG)
                    after(pe, attT_ready, r)
                    transposes(att[q], bank(4), att_xposed)
                if exists(s):
                    numerators(s, p, 1)
                    kv_products(s, p, 3)
                if exists(r):
                    pe.wait_ge(attT_ready, r + 1)
                    after(pe, x1_ready, r)
                    for t in range(TG):
                        last = nc.tensor.matmul(bank(5)[:, P * t:P * (t + 1)],
                                                attT[:, P * t:P * (t + 1)], w_o[:, :],
                                                start=True, stop=True)
                    last.then_inc(proj_done, 1)
                if exists(g):
                    pe.wait_ge(hT_ready, g + 1)
                    after(pe, phiq_ready, g)
                    nc.tensor.matmul(bank(1), w_q[:, :], hT[q][:, :], start=True, stop=True)\
                        .then_inc(q_done, 1)
                    after(pe, phik_ready, g)
                    for t in range(TG):
                        last = nc.tensor.matmul(
                            pair[3][:, t // 2, 2 * D * (t % 2):2 * D * (t % 2 + 1)],
                            hT[q][:, P * t:P * (t + 1)], w_kv[:, :], start=True, stop=True)
                    last.then_inc(kv_done, 1)
                if exists(s):
                    numerators(s, p, 2)
                    numerators(s, p, 3)

            def up(s, p, f):
                after(pe, rnd_ready, s * NF - NF + f + 1)
                nc.tensor.matmul(bank(2 + f), w_1s[:, P * f:P * (f + 1)], hT[p][:, :],
                                 start=True, stop=True).then_inc(up_done, 1)

            def phase2(s, p):
                g, q, r = s + 1, 1 - p, s - 1
                if exists(s):
                    pe.wait_ge(h2T_ready, s + 1)
                    up(s, p, 0)
                    up(s, p, 1)
                if exists(g):
                    pe.wait_ge(ln2.done, g + 1)
                    after(pe, h2T_ready, g)
                    transposes(xn[q], bank(0), h2_xposed)
                if exists(s):
                    up(s, p, 2)
                    up(s, p, 3)
                if exists(r):
                    pe.wait_ge(gel_ready, r * NF + NF)
                    after(pe, ysum_ready, r - 1)
                    for t in range(TG):
                        for f in range(NF):
                            last = nc.tensor.matmul(bank(6 + q)[:, P * t:P * (t + 1)],
                                                    gel[:, q, f, P * t:P * (t + 1)], w_2[:, f, :],
                                                    start=(f == 0), stop=(f == NF - 1))
                    last.then_inc(down_done, 1)

            def scores(n, t, p):
                if t == 0:
                    pass
                after(pe, pT_ready, n - 1)
                for half in range(2):
                    nc.tensor.matmul(pair[t % 2][:, half, :], q_bd[p][:, half, t, :],
                                     k_exp[:, p, half, t, :, :].rearrange("p h k -> p (h k)"),
                                     start=True, stop=False)
                    last = nc.tensor.matmul(pair[t % 2][:, half, :], ident_bf[:, :],
                                            causal_bf[:, :], start=False, stop=True)
                last.then_inc(s_done, 1)

            def turn_probabilities(n, t):
                flat = pair[t % 2][:, :, :].rearrange("p a c -> p (a c)")
                for i in range(HH):
                    if i % (HH // 2) == 0:
                        pe.wait_ge(exp_ready, n * 2 + (2 * i) // HH + 1)
                    last = nc.tensor.transpose(flat[:, P * i:P * (i + 1)],
                                               s_sub[t % 2][:, P * i:P * (i + 1)], ident[:, :])
                last.then_inc(p_xposed, 1)

            def weigh_values(n, t, p):
                pe.wait_ge(pT_ready, n + 1)
                after(pe, xatt_ready, n)
                for i in range(HH):
                    for b in range(2):
                        last = nc.tensor.matmul(
                            bank(7)[b * S:(b + 1) * S, 2 * HV * i:2 * HV * (i + 1)],
                            pT[t % 2][:, P * i + b * S:P * i + (b + 1) * S],
                            v2[p][:, 2 * t + b, i, :, :].rearrange("p h e -> p (h e)"),
                            start=True, stop=True)
                last.then_inc(pv_done, 1)

            def project_qk(src, w, dst, done):
                for half in range(2):
                    for b in range(2):
                        last = nc.tensor.matmul(
                            dst[b * S:(b + 1) * S, TG * S * half:TG * S * (half + 1)],
                            w[:, FH * half:FH * (half + 1)],
                            src[:, :].rearrange("p (t b k) -> p t b k", b=2, k=S)[:, :, b, :],
                            start=True, stop=True)
                last.then_inc(done, 1)

            def project_v():
                for u in range(2 * TG):
                    for h in range(2):
                        last = nc.tensor.matmul(bank(4)[h * S:(h + 1) * S, FH * u:FH * (u + 1)],
                                                cT[:, S * u:S * (u + 1)],
                                                w_xv[:, FH * h:FH * (h + 1)],
                                                start=True, stop=True)
                last.then_inc(xv_done, 1)

            def moe(g, t):
                nc.tensor.matmul(bank([4, 5, 6, 4][t])[:, 0:2 * D + NE], y2T[:, P * t:P * (t + 1)],
                                 w_moe[:, :], start=True, stop=True).then_inc(moe_done, 1)

            def phase3(s, p):
                g, q, r = s + 1, 1 - p, s - 1
                for t in range(TG):
                    if t < TG - 1 and exists(s):
                        scores(s * TG + t + 1, t + 1, p)
                    if t == TG - 1 and exists(g):
                        pe.wait_ge(kexp_ready, g + 1)
                        pe.wait_ge(qbd_ready, g + 1)
                        scores(g * TG, 0, q)
                    if t == 0 and exists(g):
                        after(pe, moe_ready, s * TG - TG)
                        after(pe, v2_ready, g)
                        after(pe, ksb_ready, g)
                        pe.wait_ge(y_copied, g + 1)
                        transposes(y_in[q], bank(4), y_xposed)
                        pe.wait_ge(ctx_loaded[q], (g - q) * 8 + 16)
                        transposes(ctx_in[q], bank(5), c_xposed)
                    if t == 1 and exists(r):
                        pe.wait_ge(xattT_ready, r + 1)
                        for u in range(TG):
                            last = nc.tensor.matmul(bank(6)[:, P * u:P * (u + 1)],
                                                    attT[:, P * u:P * (u + 1)], w_xo[:, :],
                                                    start=True, stop=True)
                        last.then_inc(xproj_done, 1)
                    if t == 2 and exists(g):
                        pe.wait_ge(qbd_ready, g + 1)
                        project_v()
                    if t == 3 and exists(r):
                        pe.wait_ge(y2T_ready, r + 1)
                        if exists(g):
                            pe.wait_ge(v2_ready, g + 1)
                            pe.wait_ge(ksb_ready, g + 1)
                        moe(r, 0)
                        moe(r, 1)
                    if exists(s):
                        turn_probabilities(s * TG + t, t)
                    if t == 0 and exists(r):
                        pe.wait_ge(xatt_ready, r * TG + TG)
                        after(pe, moe_ready, s * TG - TG)
                        transposes(att[q], bank(6), xatt_xposed)
                    if t == 1 and exists(g):
                        pe.wait_ge(yT_ready, g + 1)
                        project_qk(yT, w_xq, bank(4), xq_done)
                        pe.wait_ge(cT_ready, g + 1)
                        project_qk(cT, w_xk, bank(5), xk_done)
                    if t == 2 and exists(r):
                        pe.wait_ge(ln_b.done, r + 1)
                        transposes(y2, bank(6), y2_xposed)
                    if t == 3 and exists(r):
                        moe(r, 2)
                        pe.wait_ge(moe_ready, r * TG + 1)
                        moe(r, 3)
                    if exists(s):
                        if t == 0:
                            pe.wait_ge(v2_ready, s + 1)
                        weigh_values(s * TG + t, t, p)

            pipeline(pe, phase1)
            pe.wait_ge(x1_ready, NG)
            pe.wait_ge(att_ready, NT)
            pe.wait_ge(const_dve, 4)
            pipeline(pe, phase2)
            pe.wait_ge(ysum_ready, NG)
            pe.wait_ge(const_ready, 2)
            pipeline(pe, phase3, last=NG)


_ORDER = ["x", "ctx_1024", "mask_BxS2_ik0", "L0_attn_ln1_g", "L0_attn_ln1_b", "L0_attn_wq",
          "L0_attn_wk", "L0_attn_wv", "L0_attn_wo", "L0_attn_ln2_g", "L0_attn_ln2_b",
          "L0_attn_w1", "L0_attn_w2", "L0_xattn_WQ", "L0_xattn_WK", "L0_xattn_WV", "L0_xattn_WO",
          "L0_ffn_W_shared", "L0_ffn_W_expert", "L0_ffn_W_gate", "L0_ffn_bias"]


def kernel(**inputs):
    import concourse.bacc as bacc
    from concourse.bass_utils import run_bass_kernel_spmd

    a = {n: np.asarray(inputs[n]) for n in _ORDER}
    tokens, width = a["x"].shape[0] * a["x"].shape[1], a["x"].shape[2]
    a["x"] = a["x"].reshape(tokens, width)
    a["ctx_1024"] = a["ctx_1024"].reshape(tokens, width)
    a["mask_BxS2_ik0"] = a["mask_BxS2_ik0"].reshape(tokens // P, P).T
    for n in ("L0_attn_ln1_g", "L0_attn_ln1_b", "L0_attn_ln2_g", "L0_attn_ln2_b"):
        a[n] = a[n].reshape(width, 1)
    for n in ("L0_ffn_W_shared", "L0_ffn_W_expert"):
        a[n] = a[n].T
    a["L0_xattn_WV"] = a["L0_xattn_WV"].reshape(width, H // 2, 2, DH).transpose(0, 2, 1, 3) \
        .reshape(width, width)
    nc = bacc.Bacc("TRN2", target_bir_lowering=False, num_devices=1)
    arrays, args = {}, []
    for n in _ORDER:
        v = np.ascontiguousarray(a[n])
        arrays[f"in_{n}"] = v
        args.append(nc.dram_tensor(f"in_{n}", v.shape, mybir.dt.from_np(v.dtype),
                                   kind="ExternalInput").ap())
    args.append(nc.dram_tensor("out_rows", (tokens, width), F32, kind="ExternalOutput").ap())
    decoder_layer(nc, *args)
    r = run_bass_kernel_spmd(nc, [arrays], core_ids=[0])
    return r.results[0]["out_rows"].reshape(inputs["x"].shape)
```

```python
from contextlib import ExitStack

import numpy as np
import concourse.bass as bass
from concourse import mybir

F32 = mybir.dt.float32
BF16 = mybir.dt.bfloat16
I32 = mybir.dt.int32
ALU = mybir.AluOpType
ACT = mybir.ActivationFunctionType
AX = mybir.AxisListType

P = 128
B, S, D = 128, 64, 128
H = 16
DH = D // H
FF = 512
NF = FF // P
NT = B * S // P
TG = 4
NG = NT // TG
GW = TG * P
HV = DH + 1
HH = H // 2
FH = D // 2
NE = 7
TOPW = 8
EPS = 1e-5
DEN_EPS = 1e-6
LEVELS = 256
HALF = LEVELS // 2
QSTEP = 0.1
ROUND = 1.5 * 2.0 ** 23
NEG = -2.0 ** 32
LOWEST = -3.0e38


def decoder_layer(nc, x, ctx, mask, ln1_g, ln1_b, wq, wk, wv, wo, ln2_g, ln2_b, w1, w2,
                  xq, xk, xv, xo, w_shared_t, w_expert_t, w_gate, bias, out):
    es = ExitStack()

    def sb(name, shape, dt=F32):
        return es.enter_context(nc.sbuf_tensor(name, shape, dt))

    def pb(name, shape, dt=F32):
        return es.enter_context(nc.psum_tensor(name, shape, dt))

    def sem(name):
        return es.enter_context(nc.semaphore(name))

    x_tiles = x.rearrange("(n p) d -> p n d", p=P)
    ctx_tiles = ctx.rearrange("(n p) d -> p n d", p=P)
    out_tiles = out.rearrange("(n p) d -> p n d", p=P)

    with es:
        X = sb("X", [P, NT, D])
        X1 = sb("X1", [P, NT, D])

        w_q = sb("w_q", [P, D])
        w_kv = sb("w_kv", [P, 2 * D])
        w_o = sb("w_o", [P, D])
        w_1 = sb("w_1", [P, FF])
        w_2 = sb("w_2", [P, NF, D])
        w_xq = sb("w_xq", [P, D])
        w_xk = sb("w_xk", [P, D])
        w_xv = sb("w_xv", [P, D])
        w_xo = sb("w_xo", [P, D])
        w_moe = sb("w_moe", [P, 2 * D + NE])
        affine = sb("affine", [P, 4])
        bias_bc = sb("bias_bc", [P, D])
        mask_i = sb("mask_i", [P, NT], I32)
        row_scale = sb("row_scale", [P, NT])
        ident = sb("ident", [P, P])
        ident_bf = sb("ident_bf", [P, P], BF16)
        head_mask = sb("head_mask", [P, H, HV])
        half_mask = sb("half_mask", [P, HH])
        causal = sb("causal", [P, HH, S])
        causal_bf = sb("causal_bf", [P, HH * S], BF16)
        minus_half = sb("minus_half", [P, TG])
        minus_one = sb("minus_one", [P, TG])

        stats = sb("stats", [P, TG, 6])
        mv = [sb(f"mv{i}", [P, TG, 2]) for i in range(2)]
        veps = sb("veps", [P, TG])
        rstd = [sb(f"rstd{i}", [P, TG]) for i in range(2)]
        negm = sb("negm", [P, TG])
        offs = [sb(f"offs{i}", [P, TG]) for i in range(2)]
        stats_b = sb("stats_b", [P, TG, 6])
        mv_b = sb("mv_b", [P, TG, 2])
        veps_b = sb("veps_b", [P, TG])
        rstd_b = [sb(f"rstd_b{i}", [P, TG]) for i in range(2)]
        negm_b = sb("negm_b", [P, TG])
        offs_b = [sb(f"offs_b{i}", [P, TG]) for i in range(2)]
        stats_c = sb("stats_c", [P, TG, 6])
        mv_c = sb("mv_c", [P, TG, 2])
        veps_c = sb("veps_c", [P, TG])
        rstd_c = sb("rstd_c", [P, TG])
        xn = [sb(f"xn{i}", [P, TG, D]) for i in range(2)]
        hT = [sb(f"hT{i}", [P, GW]) for i in range(2)]
        att = [sb(f"att{i}", [P, TG, D]) for i in range(2)]
        attT = sb("attT", [P, GW])
        den = sb("den", [P, 2 * H])
        rec = sb("rec", [P, 2 * H])
        expqk = [sb(f"expqk{i}", [P, 2, GW]) for i in range(2)]
        phi_q = [sb(f"phi_q{i}", [P, GW]) for i in range(2)]
        phi_k = [sb(f"phi_k{i}", [P, TG, D]) for i in range(2)]
        v_ext = [sb(f"v_ext{i}", [P, TG, 2, H * HV]) for i in range(2)]
        kv_m = [sb(f"kv_m{i}", [P, 2, H * HV]) for i in range(2)]
        rnd = [sb(f"rnd{i}", [P, GW]) for i in range(2)]
        lev = [sb(f"lev{i}", [P, GW], BF16) for i in range(2)]
        gel = sb("gel", [P, 2, NF, GW])
        k_exp = X1[:, :, :].rearrange("p n d -> p (n d)").rearrange(
            "p (q g t h k) -> p q g t h k", q=2, g=2, t=TG, h=HH)
        big = gel[:, :, :, :].rearrange("p q f n -> p (q f n)")
        s_sub = [big[:, 1024 * i:1024 * (i + 1)] for i in range(2)]
        pT = [big[:, 2048 + 1024 * i:2048 + 1024 * (i + 1)] for i in range(2)]
        ctx_in = [sb(f"ctx_in{i}", [P, TG, D]) for i in range(2)]
        y_in = xn
        yT = hT[0]
        cT = hT[1]
        q_bd = [sb(f"q_bd{i}", [P, 2, TG, P]) for i in range(2)]
        k_sb = sb("k_sb", [P, 2, TG, S])
        v2 = [sb(f"v2{i}", [P, 2 * TG, HH, 2, HV]) for i in range(2)]
        neg_max = [sb(f"neg_max{i}", [P, H]) for i in range(2)]
        y2 = sb("y2", [P, TG, D])
        y2b = sb("y2b", [P, TG, D])
        y2T = sb("y2T", [P, GW])
        moe_s = [sb(f"moe_s{i}", [P, TG, D]) for i in range(2)]
        moe_e = [sb(f"moe_e{i}", [P, TG, D + TOPW]) for i in range(2)]
        top = sb("top", [P, TG, TOPW])
        top_e = sb("top_e", [P, TG, TOPW])
        top_z = sb("top_z", [P, TG])
        top_p = sb("top_p", [P, TG, 2])
        top_s = sb("top_s", [P, TG])
        top_w = sb("top_w", [P, TG, 2])
        top_sum = sb("top_sum", [P, TG])

        pair = [pb(f"pair{i}", [P, 2, 512]) for i in range(4)]

        def bank(i):
            return pair[i // 2][:, i % 2, :]

        w1_loaded, w_loaded = sem("w1_loaded"), sem("w_loaded")
        x_loaded = [sem(f"x_loaded{i}") for i in range(2)]
        ctx_loaded = [sem(f"ctx_loaded{i}") for i in range(2)]
        out_stored = sem("out_stored")
        const_step, const_ready, const_dve = sem("const_step"), sem("const_ready"), sem("const_dve")

        passed = {e.engine: sem(f"passed_{n}") for n, e in
                  (("act", nc.scalar), ("dve", nc.vector), ("pool", nc.gpsimd))}

        class Norm:
            def __init__(self, name):
                self.stats, self.mv, self.eps, self.rstd, self.offs, self.done = (
                    sem(f"{name}_{n}") for n in ("stats", "mv", "eps", "rstd", "offs", "done"))

        ln1, ln2, ln_a, ln_b, ln_c = (Norm(n) for n in ("ln1", "ln2", "ln_a", "ln_b", "ln_c"))
        xn_xposed, hT_ready = sem("xn_xposed"), sem("hT_ready")
        q_done, kv_done = sem("q_done"), sem("kv_done")
        expq_ready, expk_ready, v_ready = sem("expq_ready"), sem("expk_ready"), sem("v_ready")
        minq_ready, mink_ready = sem("minq_ready"), sem("mink_ready")
        phiq_ready, phik_ready = sem("phiq_ready"), sem("phik_ready")
        kvsum_done, kvm_ready, num_done = sem("kvsum_done"), sem("kvm_ready"), sem("num_done")
        den_ready, rec_ready, att_ready = sem("den_ready"), sem("rec_ready"), sem("att_ready")
        att_xposed, attT_ready, proj_done = sem("att_xposed"), sem("attT_ready"), sem("proj_done")
        x1_ready, xs_ready = sem("x1_ready"), sem("xs_ready")
        h2_xposed, h2T_ready = sem("h2_xposed"), sem("h2T_ready")
        up_done, rnd_ready, lev_ready, gel_ready = (sem(n) for n in
            ("up_done", "rnd_ready", "lev_ready", "gel_ready"))
        low_ready = sem("low_ready")
        down_done, ysum_ready = sem("down_done"), sem("ysum_ready")
        y_copied, y_xposed, c_xposed, yT_ready, cT_ready = (sem(n) for n in
            ("y_copied", "y_xposed", "c_xposed", "yT_ready", "cT_ready"))
        xq_done, xk_done, qbd_ready, ksb_ready, kexp_ready = (sem(n) for n in
            ("xq_done", "xk_done", "qbd_ready", "ksb_ready", "kexp_ready"))
        kexp_act_ready = sem("kexp_act_ready")
        xv_done, v2_ready = sem("xv_done"), sem("v2_ready")
        s_done, max_ready, sub_ready, exp_ready = (sem(n) for n in
            ("s_done", "max_ready", "sub_ready", "exp_ready"))
        p_xposed, pT_ready, pv_done = sem("p_xposed"), sem("pT_ready"), sem("pv_done")
        xrec_ready, xatt_ready, xatt_xposed, xattT_ready = (sem(n) for n in
            ("xrec_ready", "xatt_ready", "xatt_xposed", "xattT_ready"))
        xproj_done, y1_ready, y2_xposed, y2T_ready, y2b_ready = (sem(n) for n in
            ("xproj_done", "y1_ready", "y2_xposed", "y2T_ready", "y2b_ready"))
        moe_done, moe_ready = sem("moe_done"), sem("moe_ready")
        top_ready, topd_ready, tope_ready, gate_step, osum_ready = (sem(n) for n in
            ("top_ready", "topd_ready", "tope_ready", "gate_step", "osum_ready"))

        block = es.enter_context(nc.Block())

        def after(eng, semaphore, count):
            if not isinstance(count, int) or count > 0:
                eng.wait_ge(semaphore, count)

        def apart(eng):
            eng.sem_inc(passed[eng.engine])

        def early(s):
            return isinstance(s, int) and s < 0

        def next_phase(s):
            return s + 2 - NG if isinstance(s, int) and NG <= s + 2 < NG + 2 else None

        def pipeline(eng, step, first=-1, last=NG):
            for s in range(first, 2):
                step(s, s % 2)
            with eng.Fori(1, NG // 2 - 1) as i:
                step(i * 2, 0)
                step(i * 2 + 1, 1)
            for s in range(NG - 2, last + 1):
                step(s, s % 2)

        def exists(g):
            return not isinstance(g, int) or 0 <= g < NG

        def tiles(g):
            return bass.ds(g * TG, TG)

        def ln_statistics(dve, ln, g, rows, stats, mv, used, count):
            after(dve, ln.mv, g)
            apart(dve)
            for t in range(TG):
                last = nc.vector.bn_stats(stats[:, t, :], rows(t))
            last.then_inc(ln.stats, 1)
            dve.wait_ge(ln.stats, g + 1)
            apart(dve)
            after(dve, used, count)
            apart(dve)
            for t in range(TG):
                last = nc.vector.bn_aggr(mv[:, t, :], stats[:, t, :])
            last.then_inc(ln.mv, 1)

        def ln_deviation(pool, ln, g, mv, veps, rstd):
            after(pool, ln.rstd, g)
            pool.wait_ge(ln.mv, g + 1)
            apart(pool)
            nc.gpsimd.tensor_scalar(veps[:, :], mv[:, :, 1], EPS, None, ALU.add).then_inc(ln.eps, 1)
            pool.wait_ge(ln.eps, g + 1)
            nc.gpsimd.tensor_tensor(rstd[:, :], veps[:, :], minus_half[:, :], ALU.pow)\
                .then_inc(ln.rstd, 1)

        def ln_offset(pool, ln, g, mv, negm, rstd, offs):
            nc.gpsimd.tensor_tensor(negm[:, :], mv[:, :, 0], minus_one[:, :], ALU.mult)\
                .then_inc(ln.offs, 1)
            pool.wait_ge(ln.rstd, g + 1)
            pool.wait_ge(ln.offs, g * 2 + 1)
            nc.gpsimd.tensor_tensor(offs[:, :], negm[:, :], rstd[:, :], ALU.mult)\
                .then_inc(ln.offs, 1)

        def ln_rows_act(act, ln, g, rows, outs, rstd, offs):
            act.wait_ge(ln.offs, g * 2 + 2)
            apart(act)
            for t in range(TG):
                last = nc.scalar.activation(outs(t), rows(t), ACT.Identity, bias=offs[:, t:t + 1],
                                            scale=rstd[:, t:t + 1])
            last.then_inc(ln.done, 1)

        def ln_rows(dve, ln, g, rows, outs, mv, rstd):
            dve.wait_ge(ln.rstd, g + 1)
            for t in range(TG):
                last = nc.vector.tensor_scalar(outs(t), rows(t), mv[:, t, 0:1], rstd[:, t:t + 1],
                                               ALU.subtract, ALU.mult)
            last.then_inc(ln.done, 1)

        weights1_sp = [(w_kv[:, 0:D], wk), (w_kv[:, D:2 * D], wv), (w_o[:, :], wo)]
        weights1_act = [(affine[:, 0:1], ln1_g), (affine[:, 1:2], ln1_b), (w_q[:, :], wq)]
        weights = [(affine[:, 2:3], ln2_g), (affine[:, 3:4], ln2_b), (w_1[:, :], w1),
                   (w_2[:, :, :], w2.rearrange("(f p) d -> p f d", p=P)),
                   (w_xq[:, :], xq), (w_xk[:, :], xk), (w_xv[:, :], xv), (w_xo[:, :], xo),
                   (w_moe[:, 0:D], w_shared_t), (w_moe[:, D:2 * D], w_expert_t),
                   (w_moe[:, 2 * D:], w_gate), (bias_bc[:, :], bias.partition_broadcast(P)),
                   (mask_i[:, :], mask)]
        PHASE1_WEIGHTS = 16 * (len(weights1_sp) + len(weights1_act))
        ALL_WEIGHTS = 16 * len(weights)

        @block.sync
        def _(sp):
            def load_x(g, p):
                sp.dma_start(X[:, tiles(g), :], x_tiles[:, tiles(g), :]).then_inc(x_loaded[p], 16)

            def load_ctx(g, p):
                sp.dma_start(ctx_in[p][:, :, :], ctx_tiles[:, tiles(g), :])\
                    .then_inc(ctx_loaded[p], 16)

            def store(g):
                sp.wait_ge(ln_c.done, g + 1)
                sp.dma_start(out_tiles[:, tiles(g), :], X[:, tiles(g), :]).then_inc(out_stored, 16)

            load_x(0, 0)
            for dst, src in weights1_sp:
                sp.dma_start(dst, src).then_inc(w1_loaded, 16)
            load_x(1, 1)
            for dst, src in weights:
                sp.dma_start(dst, src).then_inc(w_loaded, 16)
            with sp.Fori(1, NG // 2) as i:
                for p in range(2):
                    sp.wait_ge(x_loaded[p], i * 16)
                    load_x(i * 2 + p, p)
            load_ctx(0, 0)
            load_ctx(1, 1)

            def turn(g, p):
                sp.wait_ge(c_xposed, g - 1)
                load_ctx(g, p)

            for g in range(2, 6):
                turn(g, g % 2)
            with sp.Fori(3, NG // 2) as i:
                for p in range(2):
                    turn(i * 2 + p, p)
                    store(i * 2 + (p - 6))
            for g in range(NG - 6, NG):
                store(g)
            sp.wait_ge(out_stored, 16 * NG)

        @block.gpsimd
        def _(pool):
            count = 0

            def const(op):
                nonlocal count
                count += 1
                op.then_inc(const_step, 1)
                pool.wait_ge(const_step, count)

            def deviation1(g, p):
                ln_deviation(pool, ln1, g, mv[p], veps, rstd[p])
                ln_offset(pool, ln1, g, mv[p], negm, rstd[p], offs[p])

            select = nc.gpsimd.affine_select
            nc.gpsimd.memset(minus_half[:, :], -0.5)
            nc.gpsimd.memset(minus_one[:, :], -1.0)
            const(nc.gpsimd.memset(ident[:, :], 0.0))
            const(select(out=ident[:, :], in_=ident[:, :], compare_op=ALU.not_equal, fill=1.0,
                         base=0, pattern=[[-1, P]], channel_multiplier=1))
            const(nc.gpsimd.memset(head_mask[:, :, :], 1.0))
            const(select(out=head_mask[:, :, :], in_=head_mask[:, :, :], compare_op=ALU.is_ge,
                         fill=0.0, base=0, pattern=[[-DH, H], [0, HV]], channel_multiplier=1))
            const(select(out=head_mask[:, :, :], in_=head_mask[:, :, :], compare_op=ALU.is_ge,
                         fill=0.0, base=DH - 1, pattern=[[DH, H], [0, HV]], channel_multiplier=-1))
            for i in range(2):
                const(nc.gpsimd.memset(v_ext[i][:, :, :, :], 0.0))
                for b in range(2):
                    half = v_ext[i][b * S:(b + 1) * S, :, b, :].rearrange("p t (h e) -> p t h e", e=HV)
                    const(nc.gpsimd.memset(half[:, :, :, DH:HV], 1.0))
                pool.sem_inc(const_ready)
                deviation1(i, i)
            const(nc.gpsimd.memset(half_mask[:, :], 1.0))
            const(nc.gpsimd.memset(causal[:, :, :], 0.0))
            for b in range(2):
                m = half_mask[b * S:(b + 1) * S, :]
                const(select(out=m, in_=m, compare_op=ALU.is_ge, fill=0.0, base=0,
                             pattern=[[-DH, HH]], channel_multiplier=1))
                const(select(out=m, in_=m, compare_op=ALU.is_ge, fill=0.0, base=DH - 1,
                             pattern=[[DH, HH]], channel_multiplier=-1))
                c = causal[b * S:(b + 1) * S, :, :]
                const(select(out=c, in_=c, compare_op=ALU.is_ge, fill=NEG, base=0,
                             pattern=[[0, HH], [-1, S]], channel_multiplier=1))
            for i in range(2):
                const(nc.gpsimd.memset(q_bd[i][:, :, :, :], 0.0))
                const(nc.gpsimd.memset(v2[i][:, :, :, :, :], 0.0))
                for h in range(2):
                    const(nc.gpsimd.memset(v2[i][h * S:(h + 1) * S, :, :, h, DH:HV], 1.0))
                const(nc.gpsimd.memset(moe_e[i][:, :, D + NE:], LOWEST))
            pool.sem_inc(const_ready)

            def phase1(s, p):
                if exists(s - 2):
                    r = s - 2
                    pool.wait_ge(x1_ready, r + 1)
                    nc.gpsimd.tensor_tensor(X[:, tiles(r), :], X[:, tiles(r), :],
                                            X1[:, tiles(r), :], ALU.add).then_inc(xs_ready, 1)
                if exists(s + 2) and not early(s):
                    deviation1(s + 2, p)
                if next_phase(s) is not None:
                    ln_deviation(pool, ln2, next_phase(s), mv[p], veps, rstd[p])

            def phase2(s, p):
                if exists(s + 2) and not early(s):
                    ln_deviation(pool, ln2, s + 2, mv[p], veps, rstd[p])
                if exists(s - 1):
                    after(pool, ln_a.done, s - 2)
                    ln_deviation(pool, ln_a, s - 1, mv_b, veps_b, rstd_b[1 - p])
                    ln_offset(pool, ln_a, s - 1, mv_b, negm_b, rstd_b[1 - p], offs_b[1 - p])

            def copy_y(g, p):
                pool.wait_ge(ln_a.done, g + 1)
                pool.wait_ge(h2_xposed, NG - 1 if isinstance(g, int) and g == 0 else NG)
                after(pool, y_xposed, g - 1)
                apart(pool)
                nc.gpsimd.tensor_copy(y_in[p][:, :, :], X[:, tiles(g), :]).then_inc(y_copied, 1)

            def spread_k(g, q, heads):
                for h in heads:
                    last = nc.gpsimd.tensor_scalar(
                        k_exp[:, q, 1, :, h, :], k_sb[:, 1, :, :],
                        half_mask[:, h:h + 1], 0.0, ALU.mult, ALU.add)
                return last

            def phase3(s, p):
                g, q = s + 1, 1 - p
                if exists(s + 2) and not early(s):
                    copy_y(s + 2, p)
                if exists(g):
                    pool.wait_ge(ksb_ready, g + 1)
                    after(pool, s_done, g * TG - TG)
                    apart(pool)
                    spread_k(g, q, range(0, 3))
                if exists(s - 1):
                    ln_deviation(pool, ln_b, s - 1, mv_b, veps_b, rstd_b[0])
                if exists(g):
                    spread_k(g, q, range(3, HH)).then_inc(kexp_ready, 1)
                if exists(s - 1):
                    r = s - 1
                    pool.wait_ge(ln_b.done, r + 1)
                    after(pool, moe_ready, r * TG)
                    for t in range(TG):
                        last = nc.gpsimd.tensor_tensor(y2b[:, t, :], y2[:, t, :], bias_bc[:, :],
                                                       ALU.add)
                    last.then_inc(y2b_ready, 1)
                if exists(s - 2):
                    ln_deviation(pool, ln_c, s - 2, mv_c, veps_c, rstd_c)

            pipeline(pool, phase1, last=NG + 1)
            pipeline(pool, phase2, first=0, last=NG - 2)
            copy_y(0, 0)
            copy_y(1, 1)
            phase2(NG - 1, 1)
            pool.wait_ge(w_loaded, ALL_WEIGHTS)
            pool.wait_ge(ln2.done, NG)
            phase3(-1, 1)
            phase2(NG, 0)
            pool.wait_ge(ln_a.done, NG)
            pipeline(pool, phase3, first=0, last=NG + 1)

        @block.scalar
        def _(act):
            for dst, src in weights1_act:
                act.dma_start(dst, src).then_inc(w1_loaded, 16)
            nc.scalar.preload_act_table(ACT.Exp)

            def phase1(s, p):
                g, q, r = s + 1, 1 - p, s - 1
                if exists(g):
                    after(act, xn_xposed, g - 1)
                    ln_rows_act(act, ln1, g, lambda t: X[:, g * TG + t, :],
                                lambda t: xn[q][:, t, :], rstd[q], offs[q])
                    if isinstance(g, int) and g == 0:
                        act.wait_ge(w1_loaded, PHASE1_WEIGHTS)
                        act.wait_ge(const_ready, 2)
                    act.wait_ge(xn_xposed, g + 1)
                    after(act, q_done, g - 1)
                    nc.scalar.activation(hT[q][:, :], bank(0), ACT.Identity, bias=affine[:, 1:2],
                                         scale=affine[:, 0:1]).then_inc(hT_ready, 1)
                if exists(r):
                    act.wait_ge(att_xposed, r + 1)
                    after(act, proj_done, r)
                    nc.scalar.activation(attT[:, :], bank(4), ACT.Copy).then_inc(attT_ready, 1)
                if exists(g):
                    act.wait_ge(kv_done, g + 1)
                    after(act, phiq_ready, g - 1)
                    kv = pair[3][:, :, :].rearrange("p a (t c) -> p (a t) c", c=2 * D)
                    nc.scalar.activation(expqk[q][:, 1, :].rearrange("p (t d) -> p t d", d=D),
                                         kv[:, :, 0:D], ACT.Exp).then_inc(expk_ready, 1)
                    after(act, kvsum_done, g * TG - TG)
                    for b in range(2):
                        rows = slice(b * S, (b + 1) * S)
                        last = nc.scalar.activation(
                            v_ext[q][rows, :, b, :].rearrange("p t (h e) -> p t h e", e=HV)[:, :, :, 0:DH],
                            kv[rows, :, D:2 * D].rearrange("p t (h e) -> p t h e", e=DH), ACT.Copy)
                    last.then_inc(v_ready, 1)
                    act.wait_ge(q_done, g + 1)
                    nc.scalar.activation(expqk[q][:, 0, :], bank(1), ACT.Exp).then_inc(expq_ready, 1)

            def round_up(s, f):
                k = s * NF + f
                act.wait_ge(up_done, k + 1)
                after(act, low_ready, k - 1)
                nc.scalar.activation(rnd[f % 2][:, :], bank(2 + f), ACT.Copy, bias=ROUND,
                                     scale=1.0 / QSTEP).then_inc(rnd_ready, 1)

            def gelu(s, p, f):
                act.wait_ge(lev_ready, s * NF + f + 1)
                nc.scalar.activation(gel[:, p, f, :], lev[f % 2][:, :], ACT.Gelu_apprx_tanh,
                                     scale=QSTEP).then_inc(gel_ready, 1)

            def phase2(s, p):
                g, q = s + 1, 1 - p
                if exists(s):
                    round_up(s, 0)
                    round_up(s, 1)
                    after(act, down_done, s - 1)
                    for f in range(2, NF):
                        round_up(s, f)
                        gelu(s, p, f - 2)
                if exists(s - 2):
                    o = s - 2
                    ln_rows_act(act, ln_a, o, lambda t: X[:, o * TG + t, :],
                                lambda t: X[:, o * TG + t, :], rstd_b[p], offs_b[p])
                if exists(g):
                    act.wait_ge(h2_xposed, g + 1)
                    after(act, up_done, g * NF - NF)
                    nc.scalar.activation(hT[q][:, :], bank(0), ACT.Identity, bias=affine[:, 3:4],
                                         scale=affine[:, 2:3]).then_inc(h2T_ready, 1)
                if exists(s):
                    gelu(s, p, NF - 2)
                    gelu(s, p, NF - 1)

            def probabilities(n, par):
                for half in range(2):
                    act.wait_ge(sub_ready, n * 2 + half + 1)
                    apart(act)
                    part = s_sub[par][:, 512 * half:512 * (half + 1)]
                    nc.scalar.activation(part, part, ACT.Exp, scale=row_scale[:, bass.ds(n, 1)])\
                        .then_inc(exp_ready, 1)

            def copy_pT(n, par):
                act.wait_ge(p_xposed, n + 1)
                after(act, pv_done, n - 1)
                nc.scalar.activation(pT[par], pair[par][:, :, :].rearrange("p a c -> p (a c)"),
                                     ACT.Copy).then_inc(pT_ready, 1)

            def phase3(s, p):
                nxt, prev, q = s + 1, s - 1, 1 - p
                for t in range(TG):
                    if t == 0 and exists(nxt):
                        act.wait_ge(y_xposed, nxt + 1)
                        after(act, xq_done, nxt)
                        nc.scalar.activation(yT[:, :], bank(4), ACT.Copy).then_inc(yT_ready, 1)
                        act.wait_ge(c_xposed, nxt + 1)
                        after(act, xv_done, nxt)
                        nc.scalar.activation(cT[:, :], bank(5), ACT.Copy).then_inc(cT_ready, 1)
                    if exists(s):
                        copy_pT(s * TG + t, t % 2)
                    if exists(s) if t < TG - 1 else exists(nxt):
                        probabilities(s * TG + t + 1, (t + 1) % 2)
                    if t == 0 and exists(prev):
                        act.wait_ge(xatt_xposed, prev + 1)
                        after(act, xproj_done, prev)
                        nc.scalar.activation(attT[:, :], bank(6), ACT.Copy).then_inc(xattT_ready, 1)
                    if t == 0 and exists(nxt):
                        act.wait_ge(xk_done, nxt + 1)
                        after(act, kexp_ready, nxt)
                        nc.scalar.activation(k_sb[:, :, :, :].rearrange("p g t k -> p (g t k)"),
                                             bank(5), ACT.Copy).then_inc(ksb_ready, 1)
                    if t == 1 and exists(nxt):
                        act.wait_ge(xq_done, nxt + 1)
                        after(act, s_done, nxt * TG - TG)
                        for b in range(2):
                            rows = slice(b * S, (b + 1) * S)
                            last = nc.scalar.activation(
                                q_bd[q][rows, :, :, rows].rearrange("p g t k -> p (g t) k"),
                                bank(4)[rows, :].rearrange("p (n k) -> p n k", k=S), ACT.Copy)
                        last.then_inc(qbd_ready, 1)
                    if t == 2 and exists(nxt):
                        after(act, pv_done, nxt * TG - TG)
                        act.wait_ge(xv_done, nxt + 1)
                        for h in range(2):
                            rows = slice(h * S, (h + 1) * S)
                            last = nc.scalar.activation(
                                v2[q][rows, :, :, h, 0:DH],
                                bank(4)[rows, :].rearrange("p (b i e) -> p b i e", i=HH, e=DH),
                                ACT.Copy)
                        last.then_inc(v2_ready, 1)
                    if t in (0, 1) and exists(nxt):
                        act.wait_ge(ksb_ready, nxt + 1)
                        for h in (range(0, 3), range(3, HH))[t]:
                            last = nc.scalar.activation(k_exp[:, q, 0, :, h, :], k_sb[:, 0, :, :],
                                                        ACT.Copy, scale=half_mask[:, h:h + 1])
                        if t == 1:
                            last.then_inc(kexp_act_ready, 1)
                    if t == 2 and exists(prev):
                        act.wait_ge(y2_xposed, prev + 1)
                        after(act, moe_done, prev * TG)
                        nc.scalar.activation(y2T[:, :], bank(6), ACT.Copy).then_inc(y2T_ready, 1)
                    if t == TG - 1 and exists(prev):
                        act.wait_ge(topd_ready, prev + 1)
                        nc.scalar.activation(top_e[:, :, :], top[:, :, :], ACT.Exp)\
                            .then_inc(tope_ready, 1)

            pipeline(act, phase1, last=NG - 1)
            act.wait_ge(w_loaded, ALL_WEIGHTS)
            phase2(-1, 1)
            nc.scalar.preload_act_table(ACT.Gelu_apprx_tanh)
            phase1(NG, 0)
            pipeline(act, phase2, first=0, last=NG - 1)
            nc.scalar.preload_act_table(ACT.Exp)
            act.wait_ge(const_dve, 3)
            act.wait_ge(ln2.done, NG)
            act.wait_ge(const_ready, 3)
            phase2(NG, 0)
            phase3(-1, 1)
            phase2(NG + 1, 1)
            act.wait_ge(down_done, NG)
            pipeline(act, phase3, first=0, last=NG + 1)

        @block.vector
        def _(dve):
            def statistics1(g, p):
                dve.wait_ge(x_loaded[p], (g - p) * 8 + 16)
                ln_statistics(dve, ln1, g, lambda t: X[:, g * TG + t, :], stats, mv[p],
                              ln1.offs, g * 2 - 2)

            statistics1(0, 0)
            statistics1(1, 1)
            dve.wait_ge(const_ready, 1)

            def constants():
                dve.wait_ge(w_loaded, ALL_WEIGHTS)
                nc.vector.tensor_scalar(row_scale[:, :], mask_i[:, :], 0.0, float(DH) ** -0.5,
                                        ALU.is_equal, ALU.mult).then_inc(const_dve, 1)
                dve.wait_ge(const_ready, 3)
                nc.vector.tensor_copy(ident_bf[:, :], ident[:, :]).then_inc(const_dve, 1)
                nc.vector.tensor_copy(causal_bf[:, :], causal[:, :, :].rearrange("p h k -> p (h k)"))\
                    .then_inc(const_dve, 1)

            def statistics2(g, p):
                dve.wait_ge(x1_ready, g + 1)
                used = (ln1.offs, 2 * (NG - 1 + g)) if isinstance(g, int) and g < 2 \
                    else (ln2.done, g - 1)
                ln_statistics(dve, ln2, g, lambda t: X1[:, g * TG + t, :], stats, mv[p], *used)

            def kv_sum(n, t):
                dve.wait_ge(kvsum_done, n + 1)
                after(dve, num_done, n - 1)
                nc.vector.tensor_tensor(
                    kv_m[t % 2][:, :, :],
                    bank(2 + t % 2)[:, 0:2 * H * HV].rearrange("p (b c) -> p b c", b=2),
                    head_mask[:, :, :].rearrange("p h e -> p (h e)").unsqueeze(1)
                    .broadcast_to([P, 2, H * HV]), ALU.mult).then_inc(kvm_ready, 1)

            def attend(s, p, half):
                k = s * 2 + half
                dve.wait_ge(num_done, k * 2 + 2)
                if half == 0:
                    after(dve, att_xposed, s - 1)
                src = bank(5)[:, 0:2 * H * HV].rearrange("p (c e) -> p c e", e=HV)
                nc.vector.tensor_scalar(den[:, :], src[:, :, DH], DEN_EPS, None, ALU.add)\
                    .then_inc(den_ready, 1)
                dve.wait_ge(den_ready, k + 1)
                nc.vector.reciprocal(rec[:, :], den[:, :]).then_inc(rec_ready, 1)
                dve.wait_ge(rec_ready, k + 1)
                nc.vector.tensor_tensor(
                    att[p][:, 2 * half:2 * half + 2, :].rearrange("p t (h e) -> p (t h) e", e=DH),
                    src[:, :, 0:DH], rec[:, :].unsqueeze(2).broadcast_to([P, 2 * H, DH]),
                    ALU.mult).then_inc(att_ready, 1)

            def phase1(s, p):
                g, q, r = s + 1, 1 - p, s - 2
                if exists(s):
                    kv_sum(s * TG, 0)
                    kv_sum(s * TG + 1, 1)
                if exists(r):
                    dve.wait_ge(proj_done, r + 1)
                    nc.vector.tensor_tensor(X1[:, tiles(r), :], X[:, tiles(r), :],
                                            bank(4).rearrange("p (t d) -> p t d", d=D), ALU.add)\
                        .then_inc(x1_ready, 1)
                if exists(s + 2) and not early(s):
                    statistics1(s + 2, p)
                if next_phase(s) is not None:
                    statistics2(next_phase(s), p)
                if exists(s):
                    kv_sum(s * TG + 2, 2)
                    attend(s, p, 0)
                    kv_sum(s * TG + 3, 3)
                if exists(g):
                    dve.wait_ge(expk_ready, g + 1)
                    nc.vector.tensor_scalar(expqk[q][:, 1, :], expqk[q][:, 1, :], 1.0, None, ALU.min)\
                        .then_inc(mink_ready, 1)
                if exists(s):
                    attend(s, p, 1)
                if exists(g):
                    dve.wait_ge(mink_ready, g + 1)
                    dve.wait_ge(v_ready, g + 1)
                    kv = pair[3][:, :, :].rearrange("p a (t c) -> p (a t) c", c=2 * D)
                    nc.vector.scalar_tensor_tensor(
                        phi_k[q][:, :, :], kv[:, :, 0:D], 1.0,
                        expqk[q][:, 1, :].rearrange("p (t d) -> p t d", d=D), ALU.add, ALU.max)\
                        .then_inc(phik_ready, 1)
                    dve.wait_ge(expq_ready, g + 1)
                    nc.vector.tensor_scalar(expqk[q][:, 0, :], expqk[q][:, 0, :], 1.0, None, ALU.min)\
                        .then_inc(minq_ready, 1)
                    dve.wait_ge(minq_ready, g + 1)
                    after(dve, num_done, g * TG - TG)
                    nc.vector.scalar_tensor_tensor(phi_q[q][:, :], bank(1), 1.0, expqk[q][:, 0, :],
                                                   ALU.add, ALU.max).then_inc(phiq_ready, 1)

            def quantise(k, f):
                dve.wait_ge(rnd_ready, k + 1)
                after(dve, gel_ready, k - 1)
                nc.vector.tensor_scalar(lev[f % 2][:, :], rnd[f % 2][:, :], ROUND, -float(HALF),
                                        ALU.subtract, ALU.max).then_inc(low_ready, 1)
                dve.wait_ge(low_ready, k + 1)
                nc.vector.tensor_scalar(lev[f % 2][:, :], lev[f % 2][:, :], HALF - 1.0, None,
                                        ALU.min).then_inc(lev_ready, 1)


            def phase2(s, p):
                g, q, r = s + 1, 1 - p, s - 1
                if exists(s):
                    for f in range(NF // 2):
                        quantise(s * NF + f, f)
                if exists(g):
                    after(dve, h2_xposed, g - 1)
                    ln_rows(dve, ln2, g, lambda t: X1[:, g * TG + t, :], lambda t: xn[q][:, t, :],
                            mv[q], rstd[q])
                if exists(s):
                    for f in range(NF // 2, NF):
                        quantise(s * NF + f, f)
                if exists(s + 2) and not early(s):
                    statistics2(s + 2, p)
                if exists(r):
                    dve.wait_ge(down_done, r + 1)
                    dve.wait_ge(xs_ready, r + 1)
                    nc.vector.tensor_tensor(X[:, tiles(r), :], X[:, tiles(r), :],
                                            bank(6 + q).rearrange("p (t d) -> p t d", d=D), ALU.add)\
                        .then_inc(ysum_ready, 1)
                    dve.wait_ge(ysum_ready, r + 1)
                    ln_statistics(dve, ln_a, r, lambda t: X[:, r * TG + t, :], stats_b, mv_b,
                                  ln_a.offs, r * 2)

            def xattend(n, p, t):
                dve.wait_ge(pv_done, n + 1)
                src = bank(7)[:, 0:H * HV].rearrange("p (h e) -> p h e", e=HV)
                nc.vector.reciprocal(rec[:, 0:H], src[:, :, DH]).then_inc(xrec_ready, 1)
                dve.wait_ge(xrec_ready, n + 1)
                nc.vector.tensor_tensor(att[p][:, t, :].rearrange("p (h e) -> p h e", e=DH),
                                        src[:, :, 0:DH],
                                        rec[:, 0:H].unsqueeze(2).broadcast_to([P, H, DH]),
                                        ALU.mult).then_inc(xatt_ready, 1)

            def shift(n, par):
                dve.wait_ge(s_done, n + 1)
                scores = pair[par][:, :, :].rearrange("p a (h k) -> p (a h) k", k=S)
                nc.vector.tensor_reduce(neg_max[par][:, :], scores, AX.X, ALU.max, negate=True)\
                    .then_inc(max_ready, 1)
                dve.wait_ge(max_ready, n + 1)
                after(dve, p_xposed, n - 1)
                for half in range(2):
                    heads = slice(HH * half, HH * (half + 1))
                    nc.vector.tensor_tensor(
                        s_sub[par][:, 512 * half:512 * (half + 1)].rearrange("p (h k) -> p h k", k=S),
                        scores[:, heads, :],
                        neg_max[par][:, heads].unsqueeze(2).broadcast_to([P, HH, S]),
                        ALU.add).then_inc(sub_ready, 1)

            def gate_top(g, p):
                apart(dve)
                for t in range(TG):
                    last = nc.vector.max(top[:, t, :], moe_e[p][:, t, D:])
                last.then_inc(top_ready, 1)
                dve.wait_ge(top_ready, g * 2 + 1)
                nc.vector.tensor_copy(top_z[:, :], top[:, :, 0]).then_inc(top_ready, 1)
                dve.wait_ge(top_ready, g * 2 + 2)
                nc.vector.tensor_tensor(top[:, :, :], top[:, :, :],
                                        top_z[:, :].unsqueeze(2).broadcast_to([P, TG, TOPW]),
                                        ALU.subtract).then_inc(topd_ready, 1)

            def gate_weights(g):
                dve.wait_ge(tope_ready, g + 1)
                step = 0

                def chain(op):
                    nonlocal step
                    step += 1
                    op.then_inc(gate_step, 1)
                    dve.wait_ge(gate_step, g * 7 + step)

                chain(nc.vector.tensor_reduce(top_z[:, :], top_e[:, :, :], AX.X, ALU.add))
                chain(nc.vector.reciprocal(top_s[:, :], top_z[:, :]))
                chain(nc.vector.tensor_tensor(top_p[:, :, :], top_e[:, :, 0:2],
                                              top_s[:, :].unsqueeze(2).broadcast_to([P, TG, 2]),
                                              ALU.mult))
                chain(nc.vector.tensor_reduce(top_z[:, :], top_p[:, :, :], AX.X, ALU.add))
                chain(nc.vector.reciprocal(top_s[:, :], top_z[:, :]))
                chain(nc.vector.tensor_tensor(top_w[:, :, :], top_p[:, :, :],
                                              top_s[:, :].unsqueeze(2).broadcast_to([P, TG, 2]),
                                              ALU.mult))
                chain(nc.vector.tensor_reduce(top_sum[:, :], top_w[:, :, :], AX.X, ALU.add))

            def mixture(g, p):
                for t in range(TG):
                    last = nc.vector.scalar_tensor_tensor(
                        moe_s[p][:, t, :], moe_e[p][:, t, 0:D], top_sum[:, t:t + 1],
                        moe_s[p][:, t, :], ALU.mult, ALU.add)
                last.then_inc(osum_ready, 1)
                dve.wait_ge(osum_ready, g + 1)
                ln_statistics(dve, ln_c, g, lambda t: moe_s[p][:, t, :], stats_c, mv_c,
                              ln_c.done, g)

            def collect(n, t, p):
                dve.wait_ge(moe_done, n + 1)
                src = bank([4, 5, 6, 4][t])
                nc.vector.tensor_tensor(moe_s[p][:, t, :], src[:, 0:D], y2b[:, t, :], ALU.add)
                nc.vector.tensor_copy(moe_e[p][:, t, 0:D + NE], src[:, D:2 * D + NE])\
                    .then_inc(moe_ready, 1)

            def phase3(s, p):
                prev, old, q = s - 1, s - 2, 1 - p
                for t in range(TG):
                    if t == 0 and exists(old):
                        gate_weights(old)
                    if t == 2 and exists(prev):
                        after(dve, y2_xposed, prev)
                        after(dve, y2b_ready, prev)
                        ln_rows(dve, ln_b, prev, lambda t: X[:, prev * TG + t, :],
                                lambda t: y2[:, t, :], mv_b, rstd_b[0])
                    if exists(s) if t < TG - 1 else exists(s + 1):
                        shift(s * TG + t + 1, (t + 1) % 2)
                    if t == 1 and exists(prev):
                        dve.wait_ge(xproj_done, prev + 1)
                        nc.vector.tensor_tensor(X[:, tiles(prev), :], X[:, tiles(prev), :],
                                                bank(6).rearrange("p (t d) -> p t d", d=D), ALU.add)\
                            .then_inc(y1_ready, 1)
                        dve.wait_ge(y1_ready, prev + 1)
                        ln_statistics(dve, ln_b, prev, lambda t: X[:, prev * TG + t, :],
                                      stats_b, mv_b, ln_b.done, prev)
                    if t == 2 and exists(old):
                        mixture(old, p)
                    if t == 3 and exists(prev):
                        dve.wait_ge(y2b_ready, prev + 1)
                        for u in range(2):
                            collect(prev * TG + u, u, q)
                    if exists(s):
                        if t == 0:
                            after(dve, xatt_xposed, s - 1)
                        xattend(s * TG + t, p, t)
                    if t == 3 and exists(prev):
                        for u in range(2, TG):
                            collect(prev * TG + u, u, q)
                        dve.wait_ge(moe_ready, s * TG)
                        gate_top(prev, q)
                    if t == 3 and exists(old):
                        ln_rows(dve, ln_c, old, lambda t: moe_s[p][:, t, :],
                                lambda t: X[:, old * TG + t, :], mv_c, rstd_c)

            pipeline(dve, phase1, last=NG - 1)
            phase2(-1, 1)
            constants()
            phase1(NG, 0)
            phase1(NG + 1, 1)
            pipeline(dve, phase2, first=0, last=NG - 1)
            phase2(NG, 0)
            phase3(-1, 1)
            dve.wait_ge(ln_a.offs, 2 * NG)
            pipeline(dve, phase3, first=0, last=NG + 1)

        @block.tensor
        def _(pe):
            pe.wait_ge(w1_loaded, PHASE1_WEIGHTS)
            pe.wait_ge(const_ready, 1)

            def transposes(src, dst, done):
                for t in range(TG):
                    last = nc.tensor.transpose(dst[:, P * t:P * (t + 1)], src[:, t, :], ident[:, :])
                last.then_inc(done, 1)

            def kv_products(s, p, t):
                n = s * TG + t
                if t == 0:
                    pe.wait_ge(phik_ready, s + 1)
                    pe.wait_ge(v_ready, s + 1)
                after(pe, kvm_ready, n - 1)
                nc.tensor.matmul(bank(2 + t % 2)[:, 0:2 * H * HV], phi_k[p][:, t, :],
                                 v_ext[p][:, t, :, :].rearrange("p b c -> p (b c)"),
                                 start=True, stop=True).then_inc(kvsum_done, 1)

            def numerators(s, p, t):
                pe.wait_ge(kvm_ready, s * TG + t + 1)
                if t == 0:
                    pe.wait_ge(phiq_ready, s + 1)
                if t % 2 == 0:
                    after(pe, att_ready, s * 2 + t // 2)
                for b in range(2):
                    last = nc.tensor.matmul(
                        bank(5)[b * S:(b + 1) * S, H * HV * (t % 2):H * HV * (t % 2 + 1)],
                        phi_q[p][:, P * t + b * S:P * t + (b + 1) * S], kv_m[t % 2][:, b, :],
                        start=True, stop=True)
                last.then_inc(num_done, 1)

            def phase1(s, p):
                g, q, r = s + 1, 1 - p, s - 1
                if exists(s):
                    kv_products(s, p, 0)
                    kv_products(s, p, 1)
                if exists(g):
                    pe.wait_ge(ln1.done, g + 1)
                    after(pe, hT_ready, g)
                    transposes(xn[q], bank(0), xn_xposed)
                if exists(s):
                    numerators(s, p, 0)
                    kv_products(s, p, 2)
                    numerators(s, p, 1)
                if exists(r):
                    pe.wait_ge(att_ready, r * 2 + 2)
                    after(pe, x1_ready, r)
                    transposes(att[q], bank(4), att_xposed)
                if exists(s):
                    kv_products(s, p, 3)
                if exists(g):
                    pe.wait_ge(hT_ready, g + 1)
                    after(pe, phik_ready, g)
                    for t in range(TG):
                        last = nc.tensor.matmul(
                            pair[3][:, t // 2, 2 * D * (t % 2):2 * D * (t % 2 + 1)],
                            hT[q][:, P * t:P * (t + 1)], w_kv[:, :], start=True, stop=True)
                    last.then_inc(kv_done, 1)
                if exists(s):
                    numerators(s, p, 2)
                    numerators(s, p, 3)
                if exists(g):
                    after(pe, phiq_ready, g)
                    nc.tensor.matmul(bank(1), w_q[:, :], hT[q][:, :], start=True, stop=True)\
                        .then_inc(q_done, 1)
                if exists(r):
                    pe.wait_ge(attT_ready, r + 1)
                    for t in range(TG):
                        last = nc.tensor.matmul(bank(4)[:, P * t:P * (t + 1)],
                                                attT[:, P * t:P * (t + 1)], w_o[:, :],
                                                start=True, stop=True)
                    last.then_inc(proj_done, 1)

            def up(s, p, f):
                after(pe, rnd_ready, s * NF - NF + f + 1)
                nc.tensor.matmul(bank(2 + f), w_1[:, P * f:P * (f + 1)], hT[p][:, :],
                                 start=True, stop=True).then_inc(up_done, 1)

            def phase2(s, p):
                g, q, r = s + 1, 1 - p, s - 1
                if exists(s):
                    pe.wait_ge(h2T_ready, s + 1)
                    for f in range(NF):
                        if isinstance(s, int) and s == 0 and f == 2:
                            pe.wait_ge(x1_ready, NG)
                        up(s, p, f)
                for t in range(TG):
                    if t == 2 and exists(g):
                        pe.wait_ge(ln2.done, g + 1)
                        after(pe, h2T_ready, g)
                        transposes(xn[q], bank(0), h2_xposed)
                    if exists(r):
                        if t == 0:
                            pe.wait_ge(gel_ready, r * NF + NF)
                            after(pe, ysum_ready, r - 1)
                        for f in range(NF):
                            last = nc.tensor.matmul(bank(6 + q)[:, P * t:P * (t + 1)],
                                                    gel[:, q, f, P * t:P * (t + 1)], w_2[:, f, :],
                                                    start=(f == 0), stop=(f == NF - 1))
                if exists(r):
                    last.then_inc(down_done, 1)

            def scores(n, t, p):
                if t == 0:
                    pass
                after(pe, pT_ready, n - 1)
                for half in range(2):
                    nc.tensor.matmul(pair[t % 2][:, half, :], q_bd[p][:, half, t, :],
                                     k_exp[:, p, half, t, :, :].rearrange("p h k -> p (h k)"),
                                     start=True, stop=False)
                    last = nc.tensor.matmul(pair[t % 2][:, half, :], ident_bf[:, :],
                                            causal_bf[:, :], start=False, stop=True)
                last.then_inc(s_done, 1)

            def turn_probabilities(n, t):
                flat = pair[t % 2][:, :, :].rearrange("p a c -> p (a c)")
                for i in range(HH):
                    if i % (HH // 2) == 0:
                        pe.wait_ge(exp_ready, n * 2 + (2 * i) // HH + 1)
                    last = nc.tensor.transpose(flat[:, P * i:P * (i + 1)],
                                               s_sub[t % 2][:, P * i:P * (i + 1)], ident[:, :])
                last.then_inc(p_xposed, 1)

            def weigh_values(n, t, p):
                pe.wait_ge(pT_ready, n + 1)
                after(pe, xatt_ready, n)
                for i in range(HH):
                    for b in range(2):
                        last = nc.tensor.matmul(
                            bank(7)[b * S:(b + 1) * S, 2 * HV * i:2 * HV * (i + 1)],
                            pT[t % 2][:, P * i + b * S:P * i + (b + 1) * S],
                            v2[p][:, 2 * t + b, i, :, :].rearrange("p h e -> p (h e)"),
                            start=True, stop=True)
                last.then_inc(pv_done, 1)

            def project_qk(src, w, dst, done):
                for half in range(2):
                    for b in range(2):
                        last = nc.tensor.matmul(
                            dst[b * S:(b + 1) * S, TG * S * half:TG * S * (half + 1)],
                            w[:, FH * half:FH * (half + 1)],
                            src[:, :].rearrange("p (t b k) -> p t b k", b=2, k=S)[:, :, b, :],
                            start=True, stop=True)
                last.then_inc(done, 1)

            def project_v():
                for u in range(2 * TG):
                    for h in range(2):
                        last = nc.tensor.matmul(bank(4)[h * S:(h + 1) * S, FH * u:FH * (u + 1)],
                                                cT[:, S * u:S * (u + 1)],
                                                w_xv[:, FH * h:FH * (h + 1)],
                                                start=True, stop=True)
                last.then_inc(xv_done, 1)

            def moe(g, t):
                nc.tensor.matmul(bank([4, 5, 6, 4][t])[:, 0:2 * D + NE], y2T[:, P * t:P * (t + 1)],
                                 w_moe[:, :], start=True, stop=True).then_inc(moe_done, 1)

            def phase3(s, p, slots=range(TG)):
                g, q, r = s + 1, 1 - p, s - 1
                for t in slots:
                    if t < TG - 1 and exists(s):
                        scores(s * TG + t + 1, t + 1, p)
                    if t == TG - 1 and exists(g):
                        pe.wait_ge(kexp_ready, g + 1)
                        pe.wait_ge(kexp_act_ready, g + 1)
                        pe.wait_ge(qbd_ready, g + 1)
                        scores(g * TG, 0, q)
                    if t == 0 and exists(g):
                        after(pe, moe_ready, s * TG - TG)
                        after(pe, v2_ready, g)
                        after(pe, ksb_ready, g)
                        pe.wait_ge(y_copied, g + 1)
                        transposes(y_in[q], bank(4), y_xposed)
                        pe.wait_ge(ctx_loaded[q], (g - q) * 8 + 16)
                        transposes(ctx_in[q], bank(5), c_xposed)
                    if exists(s):
                        turn_probabilities(s * TG + t, t)
                    if t == 1 and exists(r):
                        pe.wait_ge(xattT_ready, r + 1)
                        for u in range(TG):
                            last = nc.tensor.matmul(bank(6)[:, P * u:P * (u + 1)],
                                                    attT[:, P * u:P * (u + 1)], w_xo[:, :],
                                                    start=True, stop=True)
                        last.then_inc(xproj_done, 1)
                    if t == 2 and exists(g):
                        pe.wait_ge(qbd_ready, g + 1)
                        project_v()
                    if t == 3 and exists(r):
                        pe.wait_ge(y2T_ready, r + 1)
                        if exists(g):
                            pe.wait_ge(v2_ready, g + 1)
                            pe.wait_ge(ksb_ready, g + 1)
                        moe(r, 0)
                        moe(r, 1)
                    if t == 0 and exists(r):
                        pe.wait_ge(xatt_ready, r * TG + TG)
                        after(pe, moe_ready, s * TG - TG)
                        transposes(att[q], bank(6), xatt_xposed)
                    if t == 0 and exists(g):
                        pe.wait_ge(cT_ready, g + 1)
                        project_qk(cT, w_xk, bank(5), xk_done)
                    if t == 1 and exists(g):
                        pe.wait_ge(yT_ready, g + 1)
                        project_qk(yT, w_xq, bank(4), xq_done)
                    if exists(s):
                        if t == 0:
                            pe.wait_ge(v2_ready, s + 1)
                        weigh_values(s * TG + t, t, p)
                    if t == 2 and exists(r):
                        pe.wait_ge(ln_b.done, r + 1)
                        transposes(y2, bank(6), y2_xposed)
                    if t == 3 and exists(r):
                        moe(r, 2)
                        pe.wait_ge(moe_ready, r * TG + 1)
                        moe(r, 3)

            pipeline(pe, phase1, last=NG - 1)
            pe.wait_ge(phiq_ready, NG)
            phase2(-1, 1)
            phase1(NG, 0)
            pe.wait_ge(att_ready, 2 * NG)
            pe.wait_ge(w_loaded, ALL_WEIGHTS)
            pipeline(pe, phase2, first=0, last=NG - 1)
            pe.wait_ge(rnd_ready, NF * NG)
            pe.wait_ge(const_ready, 3)
            pe.wait_ge(const_dve, 3)
            phase3(-1, 1, slots=(0, 1))
            phase2(NG, 0)
            phase3(-1, 1, slots=range(2, TG))
            pe.wait_ge(ysum_ready, NG)
            pipeline(pe, phase3, first=0, last=NG)


_ORDER = ["x", "ctx_1024", "mask_BxS2_ik0", "L0_attn_ln1_g", "L0_attn_ln1_b", "L0_attn_wq",
          "L0_attn_wk", "L0_attn_wv", "L0_attn_wo", "L0_attn_ln2_g", "L0_attn_ln2_b",
          "L0_attn_w1", "L0_attn_w2", "L0_xattn_WQ", "L0_xattn_WK", "L0_xattn_WV", "L0_xattn_WO",
          "L0_ffn_W_shared", "L0_ffn_W_expert", "L0_ffn_W_gate", "L0_ffn_bias"]


def kernel(**inputs):
    import concourse.bacc as bacc
    from concourse.bass_utils import run_bass_kernel_spmd

    a = {n: np.asarray(inputs[n]) for n in _ORDER}
    tokens, width = a["x"].shape[0] * a["x"].shape[1], a["x"].shape[2]
    a["x"] = a["x"].reshape(tokens, width)
    a["ctx_1024"] = a["ctx_1024"].reshape(tokens, width)
    a["mask_BxS2_ik0"] = a["mask_BxS2_ik0"].reshape(tokens // P, P).T
    for n in ("L0_attn_ln1_g", "L0_attn_ln1_b", "L0_attn_ln2_g", "L0_attn_ln2_b"):
        a[n] = a[n].reshape(width, 1)
    for n in ("L0_ffn_W_shared", "L0_ffn_W_expert"):
        a[n] = a[n].T
    a["L0_xattn_WV"] = a["L0_xattn_WV"].reshape(width, H // 2, 2, DH).transpose(0, 2, 1, 3) \
        .reshape(width, width)
    nc = bacc.Bacc("TRN2", target_bir_lowering=False, num_devices=1)
    arrays, args = {}, []
    for n in _ORDER:
        v = np.ascontiguousarray(a[n])
        arrays[f"in_{n}"] = v
        args.append(nc.dram_tensor(f"in_{n}", v.shape, mybir.dt.from_np(v.dtype),
                                   kind="ExternalInput").ap())
    args.append(nc.dram_tensor("out_rows", (tokens, width), F32, kind="ExternalOutput").ap())
    decoder_layer(nc, *args)
    r = run_bass_kernel_spmd(nc, [arrays], core_ids=[0])
    return r.results[0]["out_rows"].reshape(inputs["x"].shape)
```

```python
from contextlib import ExitStack

import numpy as np
import concourse.bass as bass
from concourse import mybir

F32 = mybir.dt.float32
BF16 = mybir.dt.bfloat16
I32 = mybir.dt.int32
F32R = mybir.dt.float32r
ALU = mybir.AluOpType
ACT = mybir.ActivationFunctionType
AX = mybir.AxisListType

P = 128
B, S, D = 128, 64, 128
H = 16
DH = D // H
FF = 512
NF = FF // P
NT = B * S // P
TG = 4
NG = NT // TG
GW = TG * P
TURN = 4
HV = DH + 1
HH = H // 2
FH = D // 2
HDMA = 5
KEXP = 4 * HH * TG * S
KDMA = 2 * HDMA * 16
NE = 7
TOPW = 8
EPS = 1e-5
DEN_EPS = 1e-6
LEVELS = 256
HALF = LEVELS // 2
QSTEP = 0.1
ROUND = 1.5 * 2.0 ** 23
NEG = -2.0 ** 32
LOWEST = -3.0e38


def decoder_layer(nc, x, ctx, mask, ln1_g, ln1_b, wq, wk, wv, wo, ln2_g, ln2_b, w1, w2,
                  xq, xk, xv, xo, w_shared_t, w_expert_t, w_gate, bias, out):
    es = ExitStack()

    def sb(name, shape, dt=F32):
        return es.enter_context(nc.sbuf_tensor(name, shape, dt))

    def pb(name, shape, dt=F32):
        return es.enter_context(nc.psum_tensor(name, shape, dt))

    def sem(name):
        return es.enter_context(nc.semaphore(name))

    x_tiles = x.rearrange("(n p) d -> p n d", p=P)
    ctx_tiles = ctx.rearrange("(n p) d -> p n d", p=P)
    out_tiles = out.rearrange("(n p) d -> p n d", p=P)

    with es:
        X = sb("X", [P, NT, D])

        w_q = sb("w_q", [P, D])
        w_kv = sb("w_kv", [P, 2 * D])
        w_o = sb("w_o", [P, D])
        w_1 = sb("w_1", [P, FF])
        w_2 = sb("w_2", [P, NF, D])
        w_xq = sb("w_xq", [P, D])
        w_xk = sb("w_xk", [P, D])
        w_xv = sb("w_xv", [P, D])
        w_xo = sb("w_xo", [P, D])
        w_moe = sb("w_moe", [P, 2 * D + NE])
        affine = sb("affine", [P, 4])
        bias_bc = sb("bias_bc", [P, D])
        mask_i = sb("mask_i", [P, NT], I32)
        row_scale = sb("row_scale", [P, NT])
        ident = sb("ident", [P, P])
        ident_bf = sb("ident_bf", [P, P], BF16)
        head_mask = sb("head_mask", [P, H, HV])
        half_mask = sb("half_mask", [P, HH])
        causal = sb("causal", [P, HH, S])
        causal_bf = sb("causal_bf", [P, HH * S], BF16)
        minus_half = sb("minus_half", [P, TG])
        minus_one = sb("minus_one", [P, TG])

        stats = sb("stats", [P, TG, 6])
        mv = [sb(f"mv{i}", [P, TG, 2]) for i in range(2)]
        veps = sb("veps", [P, TG])
        rstd = [sb(f"rstd{i}", [P, TG]) for i in range(2)]
        stats_b = sb("stats_b", [P, TG, 6])
        mv_b = sb("mv_b", [P, TG, 2])
        veps_b = sb("veps_b", [P, TG])
        rstd_b = [sb(f"rstd_b{i}", [P, TG]) for i in range(2)]
        negm_b = sb("negm_b", [P, TG])
        offs_b = [sb(f"offs_b{i}", [P, TG]) for i in range(2)]
        stats_c = sb("stats_c", [P, TG, 6])
        mv_c = sb("mv_c", [P, TG, 2])
        veps_c = sb("veps_c", [P, TG])
        rstd_c = sb("rstd_c", [P, TG])
        negm_c = sb("negm_c", [P, TG])
        offs_c = sb("offs_c", [P, TG])
        xn = [sb(f"xn{i}", [P, TG, D]) for i in range(2)]
        hT = [sb(f"hT{i}", [P, GW]) for i in range(2)]
        att = [sb(f"att{i}", [P, TG, D]) for i in range(2)]
        attT = sb("attT", [P, GW])
        proj_sb = sb("proj_sb", [P, TG, D])
        den = sb("den", [P, 2 * H])
        rec = sb("rec", [P, 2 * H])
        rnd = [sb(f"rnd{i}", [P, GW]) for i in range(2)]
        lev = [sb(f"lev{i}", [P, GW], BF16) for i in range(2)]
        gel = sb("gel", [P, 2, NF, GW])
        big = gel[:, :, :, :].rearrange("p q f n -> p (q f n)")
        s_sub = [big[:, 1024 * i:1024 * (i + 1)] for i in range(2)]
        pT = [big[:, 2048 + 1024 * i:2048 + 1024 * (i + 1)] for i in range(2)]
        ctx_in = [sb(f"ctx_in{i}", [P, TG, D]) for i in range(2)]
        y_in = xn
        yT = hT[0]
        cT = hT[1]
        q_bd = [sb(f"q_bd{i}", [P, 2, 2 * TG, P], F32R) for i in range(2)]
        k_sb = sb("k_sb", [P, 2, 2 * TG * S], F32R)
        v2 = [sb(f"v2{i}", [P, 2 * TG, HH, 2, HV]) for i in range(2)]
        neg_max = [sb(f"neg_max{i}", [P, H]) for i in range(2)]
        y2 = sb("y2", [P, TG, D])
        y2b = sb("y2b", [P, TG, D])
        y2T = sb("y2T", [P, GW])
        moe_s = [sb(f"moe_s{i}", [P, TG, D]) for i in range(2)]
        moe_e = [sb(f"moe_e{i}", [P, TG, D + TOPW]) for i in range(2)]
        top = sb("top", [P, TG, TOPW])
        top_e = sb("top_e", [P, TG, TOPW])
        top_z = sb("top_z", [P, TG])
        top_p = sb("top_p", [P, TG, 2])
        top_s = sb("top_s", [P, TG])
        top_w = sb("top_w", [P, TG, 2])
        top_sum = sb("top_sum", [P, TG])

        with ExitStack() as early_memory:
            X1 = early_memory.enter_context(nc.sbuf_tensor("X1", [P, NT, D], F32))
            arena = early_memory.enter_context(nc.sbuf_tensor("arena", [P, KEXP], F32))
        k_exp = [sb(f"k_exp{i}", [P, 4, HH, TG * S], F32R) for i in (1, 0)][::-1]
        used = 0

        def part(*shape):
            nonlocal used
            size = int(np.prod(shape))
            used += size
            flat = arena[:, used - size:used]
            names = "abc"[:len(shape)]
            if len(shape) == 1:
                return flat
            return flat.rearrange(f"p ({' '.join(names)}) -> p {' '.join(names)}",
                                  **{n: d for n, d in zip(names, shape)})

        expqk = [part(2, GW) for _ in range(2)]
        phi_q = [part(GW) for _ in range(2)]
        phi_k = [part(TG, D) for _ in range(2)]
        v_ext = [part(TG, 2, H * HV) for _ in range(2)]
        kv_m = [part(2, H * HV) for _ in range(2)]

        pair = [pb(f"pair{i}", [P, 2, 512]) for i in range(4)]

        def bank(i):
            return pair[i // 2][:, i % 2, :]

        w1_loaded, w_loaded = sem("w1_loaded"), sem("w_loaded")
        x_loaded = [sem(f"x_loaded{i}") for i in range(2)]
        ctx_loaded = [sem(f"ctx_loaded{i}") for i in range(2)]
        out_stored = sem("out_stored")
        const_step, const_ready, const_dve = sem("const_step"), sem("const_ready"), sem("const_dve")

        passed = {e.engine: sem(f"passed_{n}") for n, e in
                  (("act", nc.scalar), ("dve", nc.vector), ("pool", nc.gpsimd), ("sp", nc.sync))}

        class Norm:
            def __init__(self, name):
                self.stats, self.mv, self.eps, self.rstd, self.offs, self.done = (
                    sem(f"{name}_{n}") for n in ("stats", "mv", "eps", "rstd", "offs", "done"))

        ln1, ln2, ln_a, ln_b, ln_c = (Norm(n) for n in ("ln1", "ln2", "ln_a", "ln_b", "ln_c"))
        xn_xposed, hT_ready = sem("xn_xposed"), sem("hT_ready")
        q_done, kv_done = sem("q_done"), sem("kv_done")
        expq_ready, expk_ready, v_ready = sem("expq_ready"), sem("expk_ready"), sem("v_ready")
        negq_ready, mink_ready = sem("negq_ready"), sem("mink_ready")
        phiq_ready, phik_ready = sem("phiq_ready"), sem("phik_ready")
        kvsum_done, kvm_ready, num_done = sem("kvsum_done"), sem("kvm_ready"), sem("num_done")
        den_ready, rec_ready, att_ready = sem("den_ready"), sem("rec_ready"), sem("att_ready")
        att_xposed, attT_ready, proj_done = sem("att_xposed"), sem("attT_ready"), sem("proj_done")
        projsb_ready = sem("projsb_ready")
        x1_ready, xs_ready = sem("x1_ready"), sem("xs_ready")
        h2_xposed, h2T_ready = sem("h2_xposed"), sem("h2T_ready")
        up_done, rnd_ready, lev_ready, gel_ready = (sem(n) for n in
            ("up_done", "rnd_ready", "lev_ready", "gel_ready"))
        low_ready = sem("low_ready")
        down_done, ysum_ready = sem("down_done"), sem("ysum_ready")
        y_copied, y_xposed, c_xposed, yT_ready, cT_ready = (sem(n) for n in
            ("y_copied", "y_xposed", "c_xposed", "yT_ready", "cT_ready"))
        xq_done, xk_done, qhigh_ready, qlow_ready, khigh_ready, klow_ready = (sem(n) for n in
            ("xq_done", "xk_done", "qhigh_ready", "qlow_ready", "khigh_ready", "klow_ready"))
        zeroed = sem("zeroed")
        kexp_ready = sem("kexp_ready")
        kexp_loaded = [sem(f"kexp_loaded{i}") for i in range(2)]
        xv_done, v2_ready = sem("xv_done"), sem("v2_ready")
        s_done, max_ready, sub_ready, exp_ready = (sem(n) for n in
            ("s_done", "max_ready", "sub_ready", "exp_ready"))
        p_xposed, pT_ready, pv_done = sem("p_xposed"), sem("pT_ready"), sem("pv_done")
        xrec_ready, xatt_ready, xatt_xposed, xattT_ready = (sem(n) for n in
            ("xrec_ready", "xatt_ready", "xatt_xposed", "xattT_ready"))
        xproj_done, y1_ready, y2_xposed, y2T_ready, y2b_ready = (sem(n) for n in
            ("xproj_done", "y1_ready", "y2_xposed", "y2T_ready", "y2b_ready"))
        moe_done, moe_ready = sem("moe_done"), sem("moe_ready")
        top_ready, topd_ready, tope_ready, gate_step, osum_ready = (sem(n) for n in
            ("top_ready", "topd_ready", "tope_ready", "gate_step", "osum_ready"))

        block = es.enter_context(nc.Block())

        def after(eng, semaphore, count):
            if not isinstance(count, int) or count > 0:
                eng.wait_ge(semaphore, count)

        def apart(eng):
            eng.sem_inc(passed[eng.engine])

        def early(s):
            return isinstance(s, int) and s < 0

        def next_phase(s):
            return s + 2 - NG if isinstance(s, int) and NG <= s + 2 < NG + 2 else None

        def pipeline(eng, step, first=-1, last=NG):
            for s in range(first, 2):
                step(s, s % 2)
            turns = (NG - 4) // TURN
            with eng.Fori(0, turns) as i:
                for k in range(TURN):
                    step(i * TURN + (2 + k), k % 2)
            for s in range(2 + turns * TURN, last + 1):
                step(s, s % 2)

        def exists(g):
            return not isinstance(g, int) or 0 <= g < NG

        def tiles(g):
            return bass.ds(g * TG, TG)

        def ln_statistics(dve, ln, g, rows, stats, mv, used, count):
            after(dve, ln.mv, g)
            apart(dve)
            for t in range(TG):
                last = nc.vector.bn_stats(stats[:, t, :], rows(t))
            last.then_inc(ln.stats, 1)
            dve.wait_ge(ln.stats, g + 1)
            apart(dve)
            after(dve, used, count)
            apart(dve)
            for t in range(TG):
                last = nc.vector.bn_aggr(mv[:, t, :], stats[:, t, :])
            last.then_inc(ln.mv, 1)

        def ln_deviation(pool, ln, g, mv, veps, rstd):
            after(pool, ln.rstd, g)
            pool.wait_ge(ln.mv, g + 1)
            apart(pool)
            nc.gpsimd.tensor_scalar(veps[:, :], mv[:, :, 1], EPS, None, ALU.add).then_inc(ln.eps, 1)
            pool.wait_ge(ln.eps, g + 1)
            nc.gpsimd.tensor_tensor(rstd[:, :], veps[:, :], minus_half[:, :], ALU.pow)\
                .then_inc(ln.rstd, 1)

        def ln_offset(pool, ln, g, mv, negm, rstd, offs):
            nc.gpsimd.tensor_tensor(negm[:, :], mv[:, :, 0], minus_one[:, :], ALU.mult)\
                .then_inc(ln.offs, 1)
            pool.wait_ge(ln.rstd, g + 1)
            pool.wait_ge(ln.offs, g * 2 + 1)
            nc.gpsimd.tensor_tensor(offs[:, :], negm[:, :], rstd[:, :], ALU.mult)\
                .then_inc(ln.offs, 1)

        def ln_rows_act(act, ln, g, rows, outs, rstd, offs):
            act.wait_ge(ln.offs, g * 2 + 2)
            apart(act)
            for t in range(TG):
                last = nc.scalar.activation(outs(t), rows(t), ACT.Identity, bias=offs[:, t:t + 1],
                                            scale=rstd[:, t:t + 1])
            last.then_inc(ln.done, 1)

        def ln_rows(dve, ln, g, rows, outs, mv, rstd):
            dve.wait_ge(ln.rstd, g + 1)
            for t in range(TG):
                last = nc.vector.tensor_scalar(outs(t), rows(t), mv[:, t, 0:1], rstd[:, t:t + 1],
                                               ALU.subtract, ALU.mult)
            last.then_inc(ln.done, 1)

        weights1_sp = [(w_kv[:, 0:D], wk), (w_kv[:, D:2 * D], wv), (w_o[:, :], wo)]
        weights1_act = [(affine[:, 0:1], ln1_g), (affine[:, 1:2], ln1_b), (w_q[:, :], wq)]
        weights = [(affine[:, 2:3], ln2_g), (affine[:, 3:4], ln2_b), (w_1[:, :], w1),
                   (w_2[:, :, :], w2.rearrange("(f p) d -> p f d", p=P)),
                   (w_xq[:, :], xq), (w_xk[:, :], xk), (w_xv[:, :], xv), (w_xo[:, :], xo),
                   (w_moe[:, 0:D], w_shared_t), (w_moe[:, D:2 * D], w_expert_t),
                   (w_moe[:, 2 * D:], w_gate), (bias_bc[:, :], bias.partition_broadcast(P)),
                   (mask_i[:, :], mask)]
        PHASE1_WEIGHTS = 16 * (len(weights1_sp) + len(weights1_act))
        ALL_WEIGHTS = 16 * len(weights)

        @block.sync
        def _(sp):
            def load_x(g, p):
                sp.dma_start(X[:, tiles(g), :], x_tiles[:, tiles(g), :]).then_inc(x_loaded[p], 16)

            def load_ctx(g, p):
                sp.dma_start(ctx_in[p][:, :, :], ctx_tiles[:, tiles(g), :])\
                    .then_inc(ctx_loaded[p], 16)

            def store(g):
                sp.wait_ge(ln_c.done, g + 1)
                sp.dma_start(out_tiles[:, tiles(g), :], X[:, tiles(g), :]).then_inc(out_stored, 16)

            load_x(0, 0)
            for dst, src in weights1_sp:
                sp.dma_start(dst, src).then_inc(w1_loaded, 16)
            load_x(1, 1)
            for dst, src in weights:
                sp.dma_start(dst, src).then_inc(w_loaded, 16)
            with sp.Fori(1, NG // 2) as i:
                for p in range(2):
                    sp.wait_ge(x_loaded[p], i * 16)
                    load_x(i * 2 + p, p)
            load_ctx(0, 0)

            def spread_k(g, q):
                sp.wait_ge(klow_ready, g + 1)
                apart(sp)
                after(sp, s_done, g * TG - TG)
                if isinstance(g, int) and g < 2:
                    sp.wait_ge(zeroed, g + 1)
                for b in range(2):
                    for h in range(HDMA):
                        rows = slice(b * S + h * DH, b * S + (h + 1) * DH)
                        sp.dma_start(k_exp[q][rows, :, h, :].bitcast(F32),
                                     k_sb[rows, :, :].bitcast(F32)
                                     .rearrange("p c (a n) -> p (c a) n", a=2))\
                            .then_inc(kexp_loaded[q], 16)

            def phase3(s, p):
                if exists(s + 1):
                    spread_k(s + 1, 1 - p)
                if exists(s + 2):
                    after(sp, c_xposed, s + 1)
                    apart(sp)
                    load_ctx(s + 2, p)
                if exists(s - 2):
                    store(s - 2)

            pipeline(sp, phase3, last=NG + 1)
            sp.wait_ge(out_stored, 16 * NG)

        @block.gpsimd
        def _(pool):
            count = 0

            def const(op):
                nonlocal count
                count += 1
                op.then_inc(const_step, 1)
                pool.wait_ge(const_step, count)

            def deviation1(g, p):
                ln_deviation(pool, ln1, g, mv[p], veps, rstd[p])

            select = nc.gpsimd.affine_select
            nc.gpsimd.memset(minus_half[:, :], -0.5)
            nc.gpsimd.memset(minus_one[:, :], -1.0)
            const(nc.gpsimd.memset(ident[:, :], 0.0))
            const(select(out=ident[:, :], in_=ident[:, :], compare_op=ALU.not_equal, fill=1.0,
                         base=0, pattern=[[-1, P]], channel_multiplier=1))
            const(nc.gpsimd.memset(head_mask[:, :, :], 1.0))
            const(select(out=head_mask[:, :, :], in_=head_mask[:, :, :], compare_op=ALU.is_ge,
                         fill=0.0, base=0, pattern=[[-DH, H], [0, HV]], channel_multiplier=1))
            const(select(out=head_mask[:, :, :], in_=head_mask[:, :, :], compare_op=ALU.is_ge,
                         fill=0.0, base=DH - 1, pattern=[[DH, H], [0, HV]], channel_multiplier=-1))
            for i in range(2):
                const(nc.gpsimd.memset(v_ext[i][:, :, :, :], 0.0))
                for b in range(2):
                    half = v_ext[i][b * S:(b + 1) * S, :, b, :].rearrange("p t (h e) -> p t h e", e=HV)
                    const(nc.gpsimd.memset(half[:, :, :, DH:HV], 1.0))
                pool.sem_inc(const_ready)
                deviation1(i, i)
            const(nc.gpsimd.memset(causal[:, :, :], 0.0))
            const(nc.gpsimd.memset(half_mask[:, :], 1.0))
            for b in range(2):
                m = half_mask[b * S:(b + 1) * S, :]
                const(select(out=m, in_=m, compare_op=ALU.is_ge, fill=0.0, base=0,
                             pattern=[[-DH, HH]], channel_multiplier=1))
                const(select(out=m, in_=m, compare_op=ALU.is_ge, fill=0.0, base=DH - 1,
                             pattern=[[DH, HH]], channel_multiplier=-1))
                c = causal[b * S:(b + 1) * S, :, :]
                const(select(out=c, in_=c, compare_op=ALU.is_ge, fill=NEG, base=0,
                             pattern=[[0, HH], [-1, S]], channel_multiplier=1))
            for i in range(2):
                const(nc.gpsimd.memset(q_bd[i][:, :, :, :].bitcast(F32), 0.0))
                const(nc.gpsimd.memset(v2[i][:, :, :, :, :], 0.0))
                for h in range(2):
                    const(nc.gpsimd.memset(v2[i][h * S:(h + 1) * S, :, :, h, DH:HV], 1.0))
                const(nc.gpsimd.memset(moe_e[i][:, :, D + NE:], LOWEST))
            pool.sem_inc(const_ready)

            def phase1(s, p):
                if exists(s + 2) and not early(s):
                    deviation1(s + 2, p)
                if next_phase(s) is not None:
                    ln_deviation(pool, ln2, next_phase(s), mv[p], veps, rstd[p])
                if exists(s - 2):
                    r = s - 2
                    pool.wait_ge(projsb_ready, r + 1)
                    apart(pool)
                    nc.gpsimd.tensor_tensor(X1[:, tiles(r), :], X[:, tiles(r), :],
                                            proj_sb[:, :, :], ALU.add).then_inc(x1_ready, 1)
                    pool.wait_ge(x1_ready, r + 1)
                    apart(pool)
                    nc.gpsimd.tensor_tensor(X[:, tiles(r), :], X[:, tiles(r), :],
                                            X1[:, tiles(r), :], ALU.add).then_inc(xs_ready, 1)

            def phase2(s, p):
                if exists(s + 2) and not early(s):
                    ln_deviation(pool, ln2, s + 2, mv[p], veps, rstd[p])
                if exists(s - 1):
                    after(pool, ln_a.done, s - 2)
                    ln_deviation(pool, ln_a, s - 1, mv_b, veps_b, rstd_b[1 - p])
                    ln_offset(pool, ln_a, s - 1, mv_b, negm_b, rstd_b[1 - p], offs_b[1 - p])

            def copy_y(g, p):
                pool.wait_ge(ln_a.done, g + 1)
                pool.wait_ge(h2_xposed, NG - 1 if isinstance(g, int) and g == 0 else NG)
                after(pool, y_xposed, g - 1)
                apart(pool)
                nc.gpsimd.tensor_copy(y_in[p][:, :, :], X[:, tiles(g), :]).then_inc(y_copied, 1)

            def spread_k(g, q, heads):
                for h in heads:
                    last = nc.gpsimd.tensor_scalar(
                        k_exp[q][:, :, h, :],
                        k_sb[:, :, :].bitcast(F32).rearrange("p c (a n) -> p (c a) n", a=2),
                        half_mask[:, h:h + 1], 0.0, ALU.mult, ALU.add)
                return last

            def zero(buffer, quarters):
                for c in quarters:
                    last = nc.gpsimd.memset(buffer[:, c, 0:HDMA, :].bitcast(F32), 0.0)
                return last

            def phase3(s, p):
                if exists(s + 2) and not early(s):
                    copy_y(s + 2, p)
                g, q = s + 1, 1 - p
                if exists(g):
                    pool.wait_ge(klow_ready, g + 1)
                    after(pool, s_done, g * TG - TG)
                    apart(pool)
                    spread_k(g, q, range(HDMA, HH - 1))
                if exists(s - 1):
                    ln_deviation(pool, ln_b, s - 1, mv_b, veps_b, rstd_b[0])
                if exists(g):
                    spread_k(g, q, range(HH - 1, HH)).then_inc(kexp_ready, 1)
                if exists(s - 1):
                    r = s - 1
                    pool.wait_ge(ln_b.done, r + 1)
                    after(pool, moe_ready, r * TG)
                    for t in range(TG):
                        last = nc.gpsimd.tensor_tensor(y2b[:, t, :], y2[:, t, :], bias_bc[:, :],
                                                       ALU.add)
                    last.then_inc(y2b_ready, 1)
                if exists(s - 2):
                    after(pool, ln_c.done, s - 2)
                    ln_deviation(pool, ln_c, s - 2, mv_c, veps_c, rstd_c)
                    ln_offset(pool, ln_c, s - 2, mv_c, negm_c, rstd_c, offs_c)

            pipeline(pool, phase1, last=NG + 1)
            for s in range(2):
                phase2(s, s)
                last = zero(k_exp[0], range(2 * s, 2 * s + 2))
            last.then_inc(zeroed, 1)
            pipeline(pool, phase2, first=2, last=NG - 2)
            copy_y(0, 0)
            copy_y(1, 1)
            phase2(NG - 1, 1)
            pool.wait_ge(w_loaded, ALL_WEIGHTS)
            phase3(-1, 1)
            phase2(NG, 0)
            pool.wait_ge(ln2.done, NG)
            zero(k_exp[1], range(4)).then_inc(zeroed, 1)
            pool.wait_ge(ln_a.done, NG)
            pipeline(pool, phase3, first=0, last=NG + 1)

        @block.scalar
        def _(act):
            for dst, src in weights1_act:
                act.dma_start(dst, src).then_inc(w1_loaded, 16)
            nc.scalar.preload_act_table(ACT.Exp)

            def rows_h(g, p):
                act.wait_ge(xn_xposed, g + 1)
                after(act, q_done, g - 1)
                nc.scalar.activation(hT[p][:, :], bank(0), ACT.Identity, bias=affine[:, 1:2],
                                     scale=affine[:, 0:1]).then_inc(hT_ready, 1)

            act.wait_ge(w1_loaded, PHASE1_WEIGHTS)
            act.wait_ge(const_ready, 2)
            rows_h(0, 0)

            def phase1(s, p):
                g, q, r = s + 1, 1 - p, s - 1
                if exists(s - 2):
                    act.wait_ge(proj_done, s - 1)
                    after(act, x1_ready, s - 2)
                    nc.scalar.activation(proj_sb[:, :, :].rearrange("p t d -> p (t d)"), bank(4),
                                         ACT.Copy).then_inc(projsb_ready, 1)
                if exists(g):
                    act.wait_ge(kv_done, g + 1)
                    after(act, phiq_ready, g - 1)
                    kv = pair[3][:, :, :].rearrange("p a (t c) -> p (a t) c", c=2 * D)
                    nc.scalar.activation(expqk[q][:, 1, :].rearrange("p (t d) -> p t d", d=D),
                                         kv[:, :, 0:D], ACT.Exp).then_inc(expk_ready, 1)
                    after(act, kvsum_done, g * TG - TG)
                    for b in range(2):
                        rows = slice(b * S, (b + 1) * S)
                        last = nc.scalar.activation(
                            v_ext[q][rows, :, b, :].rearrange("p t (h e) -> p t h e", e=HV)[:, :, :, 0:DH],
                            kv[rows, :, D:2 * D].rearrange("p t (h e) -> p t h e", e=DH), ACT.Copy)
                    last.then_inc(v_ready, 1)
                if exists(r):
                    act.wait_ge(att_xposed, r + 1)
                    after(act, proj_done, r)
                    nc.scalar.activation(attT[:, :], bank(4), ACT.Copy).then_inc(attT_ready, 1)
                if exists(g):
                    act.wait_ge(q_done, g + 1)
                    nc.scalar.activation(expqk[q][:, 0, :], bank(1), ACT.Relu, scale=-1.0)\
                        .then_inc(negq_ready, 1)
                    act.wait_ge(negq_ready, g + 1)
                    nc.scalar.activation(expqk[q][:, 0, :], expqk[q][:, 0, :], ACT.Exp,
                                         scale=-1.0).then_inc(expq_ready, 1)
                if exists(s + 2):
                    rows_h(s + 2, p)

            def round_up(s, f):
                k = s * NF + f
                act.wait_ge(up_done, k + 1)
                after(act, low_ready, k - 1)
                nc.scalar.activation(rnd[f % 2][:, :], bank(2 + f), ACT.Copy, bias=ROUND,
                                     scale=1.0 / QSTEP).then_inc(rnd_ready, 1)

            def gelu(s, p, f):
                act.wait_ge(lev_ready, s * NF + f + 1)
                nc.scalar.activation(gel[:, p, f, :], lev[f % 2][:, :], ACT.Gelu_apprx_tanh,
                                     scale=QSTEP).then_inc(gel_ready, 1)

            def phase2(s, p):
                g, q = s + 1, 1 - p
                if exists(s):
                    round_up(s, 0)
                    round_up(s, 1)
                    after(act, down_done, s - 1)
                    for f in range(2, NF):
                        round_up(s, f)
                        gelu(s, p, f - 2)
                if exists(s - 2):
                    o = s - 2
                    ln_rows_act(act, ln_a, o, lambda t: X[:, o * TG + t, :],
                                lambda t: X[:, o * TG + t, :], rstd_b[p], offs_b[p])
                if exists(g):
                    act.wait_ge(h2_xposed, g + 1)
                    after(act, up_done, g * NF - NF)
                    nc.scalar.activation(hT[q][:, :], bank(0), ACT.Identity, bias=affine[:, 3:4],
                                         scale=affine[:, 2:3]).then_inc(h2T_ready, 1)
                if exists(s):
                    gelu(s, p, NF - 2)
                    gelu(s, p, NF - 1)

            def probabilities(n, par):
                for half in range(2):
                    act.wait_ge(sub_ready, n * 2 + half + 1)
                    apart(act)
                    part = s_sub[par][:, 512 * half:512 * (half + 1)]
                    nc.scalar.activation(part, part, ACT.Exp, scale=row_scale[:, bass.ds(n, 1)])\
                        .then_inc(exp_ready, 1)

            def copy_pT(n, par):
                act.wait_ge(p_xposed, n + 1)
                after(act, pv_done, n - 1)
                nc.scalar.activation(pT[par], pair[par][:, :, :].rearrange("p a c -> p (a c)"),
                                     ACT.Copy).then_inc(pT_ready, 1)

            def phase3(s, p, slots=range(TG)):
                nxt, prev, q = s + 1, s - 1, 1 - p
                for t in slots:
                    if t == 0 and exists(nxt):
                        act.wait_ge(c_xposed, nxt + 1)
                        after(act, xv_done, nxt)
                        nc.scalar.activation(cT[:, :], bank(5), ACT.Copy).then_inc(cT_ready, 1)
                        act.wait_ge(y_xposed, nxt + 1)
                        after(act, xq_done, nxt)
                        nc.scalar.activation(yT[:, :], bank(4), ACT.Copy).then_inc(yT_ready, 1)
                    if exists(s):
                        copy_pT(s * TG + t, t % 2)
                    if t == 0 and exists(nxt):
                        act.wait_ge(xk_done, nxt + 1)
                        if exists(s):
                            act.wait_ge(kexp_ready, s + 1)
                            act.wait_ge(kexp_loaded[p], (s - p) * (KDMA // 2) + KDMA)
                        nc.scalar.activation(k_sb[:, 0, :], bank(5), ACT.Copy)\
                            .then_inc(khigh_ready, 1)
                    if t == 0 and exists(s - 2):
                        act.wait_ge(topd_ready, s - 1)
                        nc.scalar.activation(top_e[:, :, :], top[:, :, :], ACT.Exp)\
                            .then_inc(tope_ready, 1)
                    if t == 0 and exists(prev):
                        act.wait_ge(xatt_xposed, prev + 1)
                        after(act, xproj_done, prev)
                        nc.scalar.activation(attT[:, :], bank(6), ACT.Copy).then_inc(xattT_ready, 1)
                    if t == TG - 1 and exists(s - 2):
                        o = s - 2
                        ln_rows_act(act, ln_c, o, lambda t: moe_s[p][:, t, :],
                                    lambda t: X[:, o * TG + t, :], rstd_c, offs_c)
                    if exists(s) if t < TG - 1 else exists(nxt):
                        probabilities(s * TG + t + 1, (t + 1) % 2)
                    if t == 1 and exists(nxt):
                        act.wait_ge(xq_done, nxt + 1)
                        after(act, s_done, nxt * TG - TG)
                        for b in range(2):
                            rows = slice(b * S, (b + 1) * S)
                            last = nc.scalar.activation(
                                q_bd[q][rows, 0, :, rows],
                                bank(4)[rows, :].rearrange("p (n k) -> p n k", k=S), ACT.Copy)
                        last.then_inc(qhigh_ready, 1)
                    if t == 2 and exists(nxt):
                        after(act, pv_done, nxt * TG - TG)
                        act.wait_ge(xv_done, nxt + 1)
                        for h in range(2):
                            rows = slice(h * S, (h + 1) * S)
                            last = nc.scalar.activation(
                                v2[q][rows, :, :, h, 0:DH],
                                bank(4)[rows, :].rearrange("p (b i e) -> p b i e", i=HH, e=DH),
                                ACT.Copy)
                        last.then_inc(v2_ready, 1)
                    if t == 2 and exists(prev):
                        act.wait_ge(y2_xposed, prev + 1)
                        after(act, moe_done, prev * TG)
                        nc.scalar.activation(y2T[:, :], bank(6), ACT.Copy).then_inc(y2T_ready, 1)

            pipeline(act, phase1, last=NG - 2)
            act.wait_ge(w_loaded, ALL_WEIGHTS)
            phase2(-1, 1)
            phase1(NG - 1, 1)
            nc.scalar.preload_act_table(ACT.Gelu_apprx_tanh)
            phase1(NG, 0)
            phase1(NG + 1, 1)
            pipeline(act, phase2, first=0, last=NG - 1)
            nc.scalar.preload_act_table(ACT.Exp)
            act.wait_ge(const_dve, 3)
            act.wait_ge(const_ready, 3)
            phase3(-1, 1, slots=(0, 1))
            phase2(NG, 0)
            phase3(-1, 1, slots=range(2, TG))
            phase2(NG + 1, 1)
            act.wait_ge(down_done, NG)
            pipeline(act, phase3, first=0, last=NG + 1)

        @block.vector
        def _(dve):
            def statistics1(g, p):
                dve.wait_ge(x_loaded[p], (g - p) * 8 + 16)
                ln_statistics(dve, ln1, g, lambda t: X[:, g * TG + t, :], stats, mv[p],
                              ln1.done, g - 1)

            def rows1(g, p):
                after(dve, xn_xposed, g - 1)
                ln_rows(dve, ln1, g, lambda t: X[:, g * TG + t, :], lambda t: xn[p][:, t, :],
                        mv[p], rstd[p])

            for g in range(2):
                statistics1(g, g)
            rows1(0, 0)
            rows1(1, 1)
            dve.wait_ge(const_ready, 1)

            def constants():
                dve.wait_ge(w_loaded, ALL_WEIGHTS)
                nc.vector.tensor_scalar(row_scale[:, :], mask_i[:, :], 0.0, float(DH) ** -0.5,
                                        ALU.is_equal, ALU.mult).then_inc(const_dve, 1)
                dve.wait_ge(const_ready, 3)
                nc.vector.tensor_copy(ident_bf[:, :], ident[:, :]).then_inc(const_dve, 1)
                nc.vector.tensor_copy(causal_bf[:, :], causal[:, :, :].rearrange("p h k -> p (h k)"))\
                    .then_inc(const_dve, 1)

            def statistics2(g, p):
                dve.wait_ge(x1_ready, g + 1)
                used = (ln1.done, NG - 1 + g) if isinstance(g, int) and g < 2 \
                    else (ln2.done, g - 1)
                ln_statistics(dve, ln2, g, lambda t: X1[:, g * TG + t, :], stats, mv[p], *used)

            def rows2(g, p):
                ln_rows(dve, ln2, g, lambda t: X1[:, g * TG + t, :], lambda t: xn[p][:, t, :],
                        mv[p], rstd[p])

            def kv_sum(n, t):
                dve.wait_ge(kvsum_done, n + 1)
                after(dve, num_done, n - 1)
                nc.vector.tensor_tensor(
                    kv_m[t % 2][:, :, :],
                    bank(2 + t % 2)[:, 0:2 * H * HV].rearrange("p (b c) -> p b c", b=2),
                    head_mask[:, :, :].rearrange("p h e -> p (h e)").unsqueeze(1)
                    .broadcast_to([P, 2, H * HV]), ALU.mult).then_inc(kvm_ready, 1)

            def attend(s, p, half):
                k = s * 2 + half
                dve.wait_ge(num_done, k * 2 + 2)
                if half == 0:
                    after(dve, att_xposed, s - 1)
                src = bank(5)[:, 0:2 * H * HV].rearrange("p (c e) -> p c e", e=HV)
                nc.vector.tensor_scalar(den[:, :], src[:, :, DH], DEN_EPS, None, ALU.add)\
                    .then_inc(den_ready, 1)
                dve.wait_ge(den_ready, k + 1)
                nc.vector.reciprocal(rec[:, :], den[:, :]).then_inc(rec_ready, 1)
                dve.wait_ge(rec_ready, k + 1)
                nc.vector.tensor_tensor(
                    att[p][:, 2 * half:2 * half + 2, :].rearrange("p t (h e) -> p (t h) e", e=DH),
                    src[:, :, 0:DH], rec[:, :].unsqueeze(2).broadcast_to([P, 2 * H, DH]),
                    ALU.mult).then_inc(att_ready, 1)

            def phase1(s, p):
                g, q, r = s + 1, 1 - p, s - 2
                if exists(s):
                    kv_sum(s * TG, 0)
                    kv_sum(s * TG + 1, 1)
                if exists(s + 2) and not early(s):
                    statistics1(s + 2, p)
                if next_phase(s) is not None:
                    statistics2(next_phase(s), p)
                if exists(s):
                    kv_sum(s * TG + 2, 2)
                    kv_sum(s * TG + 3, 3)
                    attend(s, p, 0)
                if exists(s + 2) and not early(s):
                    rows1(s + 2, p)
                if next_phase(s) == 0:
                    after(dve, xn_xposed, NG - 1)
                    rows2(0, 0)
                if exists(g):
                    dve.wait_ge(expk_ready, g + 1)
                    nc.vector.tensor_scalar(expqk[q][:, 1, :], expqk[q][:, 1, :], 1.0, None, ALU.min)\
                        .then_inc(mink_ready, 1)
                    dve.wait_ge(mink_ready, g + 1)
                    dve.wait_ge(v_ready, g + 1)
                    kv = pair[3][:, :, :].rearrange("p a (t c) -> p (a t) c", c=2 * D)
                    nc.vector.scalar_tensor_tensor(
                        phi_k[q][:, :, :], kv[:, :, 0:D], 1.0,
                        expqk[q][:, 1, :].rearrange("p (t d) -> p t d", d=D), ALU.add, ALU.max)\
                        .then_inc(phik_ready, 1)
                if exists(s):
                    attend(s, p, 1)
                if exists(g):
                    dve.wait_ge(expq_ready, g + 1)
                    after(dve, num_done, g * TG - TG)
                    nc.vector.scalar_tensor_tensor(phi_q[q][:, :], bank(1), 1.0, expqk[q][:, 0, :],
                                                   ALU.add, ALU.max).then_inc(phiq_ready, 1)

            def quantise(k, f):
                dve.wait_ge(rnd_ready, k + 1)
                after(dve, gel_ready, k - 1)
                nc.vector.tensor_scalar(lev[f % 2][:, :], rnd[f % 2][:, :], ROUND, -float(HALF),
                                        ALU.subtract, ALU.max).then_inc(low_ready, 1)
                dve.wait_ge(low_ready, k + 1)
                nc.vector.tensor_scalar(lev[f % 2][:, :], lev[f % 2][:, :], HALF - 1.0, None,
                                        ALU.min).then_inc(lev_ready, 1)

            def phase2(s, p):
                g, q, r = s + 1, 1 - p, s - 1
                if exists(s):
                    for f in range(NF // 2):
                        quantise(s * NF + f, f)
                if exists(g):
                    after(dve, h2_xposed, g - 1)
                    rows2(g, q)
                if exists(s):
                    for f in range(NF // 2, NF):
                        quantise(s * NF + f, f)
                if exists(s + 2) and not early(s):
                    statistics2(s + 2, p)
                if exists(r):
                    dve.wait_ge(down_done, r + 1)
                    dve.wait_ge(xs_ready, r + 1)
                    nc.vector.tensor_tensor(X[:, tiles(r), :], X[:, tiles(r), :],
                                            bank(6 + q).rearrange("p (t d) -> p t d", d=D), ALU.add)\
                        .then_inc(ysum_ready, 1)
                    dve.wait_ge(ysum_ready, r + 1)
                    ln_statistics(dve, ln_a, r, lambda t: X[:, r * TG + t, :], stats_b, mv_b,
                                  ln_a.offs, r * 2)

            def xattend(n, p, t):
                dve.wait_ge(pv_done, n + 1)
                src = bank(7)[:, 0:H * HV].rearrange("p (h e) -> p h e", e=HV)
                nc.vector.reciprocal(rec[:, 0:H], src[:, :, DH]).then_inc(xrec_ready, 1)
                dve.wait_ge(xrec_ready, n + 1)
                nc.vector.tensor_tensor(att[p][:, t, :].rearrange("p (h e) -> p h e", e=DH),
                                        src[:, :, 0:DH],
                                        rec[:, 0:H].unsqueeze(2).broadcast_to([P, H, DH]),
                                        ALU.mult).then_inc(xatt_ready, 1)

            def shift(n, par):
                dve.wait_ge(s_done, n + 1)
                scores = pair[par][:, :, :].rearrange("p a (h k) -> p (a h) k", k=S)
                nc.vector.tensor_reduce(neg_max[par][:, :], scores, AX.X, ALU.max, negate=True)\
                    .then_inc(max_ready, 1)
                dve.wait_ge(max_ready, n + 1)
                after(dve, p_xposed, n - 1)
                for half in range(2):
                    heads = slice(HH * half, HH * (half + 1))
                    nc.vector.tensor_tensor(
                        s_sub[par][:, 512 * half:512 * (half + 1)].rearrange("p (h k) -> p h k", k=S),
                        scores[:, heads, :],
                        neg_max[par][:, heads].unsqueeze(2).broadcast_to([P, HH, S]),
                        ALU.add).then_inc(sub_ready, 1)

            def gate_top(g, p):
                apart(dve)
                for t in range(TG):
                    last = nc.vector.max(top[:, t, :], moe_e[p][:, t, D:])
                last.then_inc(top_ready, 1)
                dve.wait_ge(top_ready, g * 2 + 1)
                nc.vector.tensor_copy(top_z[:, :], top[:, :, 0]).then_inc(top_ready, 1)
                dve.wait_ge(top_ready, g * 2 + 2)
                nc.vector.tensor_tensor(top[:, :, :], top[:, :, :],
                                        top_z[:, :].unsqueeze(2).broadcast_to([P, TG, TOPW]),
                                        ALU.subtract).then_inc(topd_ready, 1)

            def gate_weights(g):
                dve.wait_ge(tope_ready, g + 1)
                step = 0

                def chain(op):
                    nonlocal step
                    step += 1
                    op.then_inc(gate_step, 1)
                    dve.wait_ge(gate_step, g * 7 + step)

                chain(nc.vector.tensor_reduce(top_z[:, :], top_e[:, :, :], AX.X, ALU.add))
                chain(nc.vector.reciprocal(top_s[:, :], top_z[:, :]))
                chain(nc.vector.tensor_tensor(top_p[:, :, :], top_e[:, :, 0:2],
                                              top_s[:, :].unsqueeze(2).broadcast_to([P, TG, 2]),
                                              ALU.mult))
                chain(nc.vector.tensor_reduce(top_z[:, :], top_p[:, :, :], AX.X, ALU.add))
                chain(nc.vector.reciprocal(top_s[:, :], top_z[:, :]))
                chain(nc.vector.tensor_tensor(top_w[:, :, :], top_p[:, :, :],
                                              top_s[:, :].unsqueeze(2).broadcast_to([P, TG, 2]),
                                              ALU.mult))
                chain(nc.vector.tensor_reduce(top_sum[:, :], top_w[:, :, :], AX.X, ALU.add))

            def mixture(g, p):
                for t in range(TG):
                    last = nc.vector.scalar_tensor_tensor(
                        moe_s[p][:, t, :], moe_e[p][:, t, 0:D], top_sum[:, t:t + 1],
                        moe_s[p][:, t, :], ALU.mult, ALU.add)
                last.then_inc(osum_ready, 1)
                dve.wait_ge(osum_ready, g + 1)
                ln_statistics(dve, ln_c, g, lambda t: moe_s[p][:, t, :], stats_c, mv_c,
                              ln_c.offs, g * 2)

            def k_low(g):
                dve.wait_ge(khigh_ready, g + 1)
                nc.vector.tensor_tensor(k_sb[:, 1, :], bank(5), k_sb[:, 0, :].bitcast(F32),
                                        ALU.subtract).then_inc(klow_ready, 1)

            def q_low(g, p):
                dve.wait_ge(qhigh_ready, g + 1)
                for b in range(2):
                    rows = slice(b * S, (b + 1) * S)
                    last = nc.vector.tensor_tensor(
                        q_bd[p][rows, 1, :, rows],
                        bank(4)[rows, :].rearrange("p (n k) -> p n k", k=S),
                        q_bd[p][rows, 0, :, rows].bitcast(F32), ALU.subtract)
                last.then_inc(qlow_ready, 1)

            def collect(n, t, p):
                dve.wait_ge(moe_done, n + 1)
                src = bank([4, 5, 6, 4][t])
                nc.vector.tensor_tensor(moe_s[p][:, t, :], src[:, 0:D], y2b[:, t, :], ALU.add)
                nc.vector.tensor_copy(moe_e[p][:, t, 0:D + NE], src[:, D:2 * D + NE])\
                    .then_inc(moe_ready, 1)

            def phase3(s, p, slots=range(TG)):
                prev, old, q = s - 1, s - 2, 1 - p
                for t in slots:
                    if t == 2 and exists(prev):
                        after(dve, y2_xposed, prev)
                        after(dve, y2b_ready, prev)
                        ln_rows(dve, ln_b, prev, lambda t: X[:, prev * TG + t, :],
                                lambda t: y2[:, t, :], mv_b, rstd_b[0])
                    if t == 3 and exists(prev):
                        dve.wait_ge(y2b_ready, prev + 1)
                        after(dve, ln_c.done, prev - 1)
                        for u in range(2):
                            collect(prev * TG + u, u, q)
                    if exists(s) if t < TG - 1 else exists(s + 1):
                        shift(s * TG + t + 1, (t + 1) % 2)
                    if t == 1 and exists(prev):
                        dve.wait_ge(xproj_done, prev + 1)
                        nc.vector.tensor_tensor(X[:, tiles(prev), :], X[:, tiles(prev), :],
                                                bank(6).rearrange("p (t d) -> p t d", d=D), ALU.add)\
                            .then_inc(y1_ready, 1)
                        dve.wait_ge(y1_ready, prev + 1)
                        ln_statistics(dve, ln_b, prev, lambda t: X[:, prev * TG + t, :],
                                      stats_b, mv_b, ln_b.done, prev)
                    if t == 2 and exists(old):
                        mixture(old, p)
                    if t == 0 and exists(s + 1):
                        k_low(s + 1)
                    if t == 0 and exists(old):
                        gate_weights(old)
                    if exists(s):
                        if t == 0:
                            after(dve, xatt_xposed, s - 1)
                        xattend(s * TG + t, p, t)
                    if t == 1 and exists(s + 1):
                        q_low(s + 1, q)
                    if t == 3 and exists(prev):
                        for u in range(2, TG):
                            collect(prev * TG + u, u, q)
                        dve.wait_ge(moe_ready, s * TG)
                        gate_top(prev, q)

            pipeline(dve, phase1, last=NG - 2)
            phase1(NG - 1, 1)
            constants()
            phase1(NG, 0)
            phase1(NG + 1, 1)
            pipeline(dve, phase2, first=0, last=NG - 1)
            phase3(-1, 1, slots=(0, 1))
            phase2(NG, 0)
            phase3(-1, 1, slots=(2, 3))
            dve.wait_ge(ln_a.offs, 2 * NG)
            pipeline(dve, phase3, first=0, last=NG + 1)

        @block.tensor
        def _(pe):
            pe.wait_ge(w1_loaded, PHASE1_WEIGHTS)
            pe.wait_ge(const_ready, 1)

            def transposes(src, dst, done):
                for t in range(TG):
                    last = nc.tensor.transpose(dst[:, P * t:P * (t + 1)], src[:, t, :], ident[:, :])
                last.then_inc(done, 1)

            def kv_products(s, p, t):
                n = s * TG + t
                if t == 0:
                    pe.wait_ge(phik_ready, s + 1)
                    pe.wait_ge(v_ready, s + 1)
                after(pe, kvm_ready, n - 1)
                nc.tensor.matmul(bank(2 + t % 2)[:, 0:2 * H * HV], phi_k[p][:, t, :],
                                 v_ext[p][:, t, :, :].rearrange("p b c -> p (b c)"),
                                 start=True, stop=True).then_inc(kvsum_done, 1)

            def numerators(s, p, t):
                pe.wait_ge(kvm_ready, s * TG + t + 1)
                if t == 0:
                    pe.wait_ge(phiq_ready, s + 1)
                if t % 2 == 0:
                    after(pe, att_ready, s * 2 + t // 2)
                for b in range(2):
                    last = nc.tensor.matmul(
                        bank(5)[b * S:(b + 1) * S, H * HV * (t % 2):H * HV * (t % 2 + 1)],
                        phi_q[p][:, P * t + b * S:P * t + (b + 1) * S], kv_m[t % 2][:, b, :],
                        start=True, stop=True)
                last.then_inc(num_done, 1)

            def xpose_rows(g, p):
                pe.wait_ge(ln1.done, g + 1)
                after(pe, hT_ready, g)
                transposes(xn[p], bank(0), xn_xposed)

            xpose_rows(0, 0)

            def phase1(s, p):
                g, q, r = s + 1, 1 - p, s - 1
                if exists(s):
                    kv_products(s, p, 0)
                    kv_products(s, p, 1)
                if exists(g):
                    pe.wait_ge(hT_ready, g + 1)
                    after(pe, phik_ready, g)
                    for t in range(TG):
                        last = nc.tensor.matmul(
                            pair[3][:, t // 2, 2 * D * (t % 2):2 * D * (t % 2 + 1)],
                            hT[q][:, P * t:P * (t + 1)], w_kv[:, :], start=True, stop=True)
                    last.then_inc(kv_done, 1)
                if exists(s):
                    numerators(s, p, 0)
                    kv_products(s, p, 2)
                    kv_products(s, p, 3)
                    numerators(s, p, 1)
                if exists(g):
                    after(pe, phiq_ready, g)
                    nc.tensor.matmul(bank(1), w_q[:, :], hT[q][:, :], start=True, stop=True)\
                        .then_inc(q_done, 1)
                if exists(r):
                    pe.wait_ge(att_ready, r * 2 + 2)
                    after(pe, projsb_ready, r)
                    transposes(att[q], bank(4), att_xposed)
                if exists(s):
                    numerators(s, p, 2)
                    numerators(s, p, 3)
                if exists(r):
                    pe.wait_ge(attT_ready, r + 1)
                    for t in range(TG):
                        last = nc.tensor.matmul(bank(4)[:, P * t:P * (t + 1)],
                                                attT[:, P * t:P * (t + 1)], w_o[:, :],
                                                start=True, stop=True)
                    last.then_inc(proj_done, 1)
                if exists(s + 2):
                    xpose_rows(s + 2, p)

            def up(s, p, f):
                after(pe, rnd_ready, s * NF - NF + f + 1)
                nc.tensor.matmul(bank(2 + f), w_1[:, P * f:P * (f + 1)], hT[p][:, :],
                                 start=True, stop=True).then_inc(up_done, 1)

            def phase2(s, p, blocks=range(NF)):
                g, q, r = s + 1, 1 - p, s - 1
                if exists(s):
                    pe.wait_ge(h2T_ready, s + 1)
                    for f in blocks:
                        if isinstance(s, int) and s == 0 and f == 2:
                            pe.wait_ge(projsb_ready, NG)
                        up(s, p, f)
                for t in range(TG):
                    if t == 2 and exists(g):
                        pe.wait_ge(ln2.done, g + 1)
                        after(pe, h2T_ready, g)
                        transposes(xn[q], bank(0), h2_xposed)
                    if exists(r):
                        if t == 0:
                            pe.wait_ge(gel_ready, r * NF + NF)
                            after(pe, ysum_ready, r - 1)
                        for f in range(NF):
                            last = nc.tensor.matmul(bank(6 + q)[:, P * t:P * (t + 1)],
                                                    gel[:, q, f, P * t:P * (t + 1)], w_2[:, f, :],
                                                    start=(f == 0), stop=(f == NF - 1))
                if exists(r):
                    last.then_inc(down_done, 1)

            def scores(n, t, p):
                after(pe, pT_ready, n - 1)
                for half in range(2):
                    for qpart, kpart in ((0, 0), (0, 1), (1, 0)):
                        nc.tensor.matmul(
                            pair[t % 2][:, half, :],
                            q_bd[p][:, qpart, half * TG + t, :],
                            k_exp[p][:, 2 * kpart + half, :, t * S:(t + 1) * S],
                            start=(qpart + kpart == 0), stop=False)
                    last = nc.tensor.matmul(pair[t % 2][:, half, :], ident_bf[:, :],
                                            causal_bf[:, :], start=False, stop=True)
                last.then_inc(s_done, 1)

            def turn_probabilities(n, t):
                flat = pair[t % 2][:, :, :].rearrange("p a c -> p (a c)")
                for i in range(HH):
                    if i % (HH // 2) == 0:
                        pe.wait_ge(exp_ready, n * 2 + (2 * i) // HH + 1)
                    last = nc.tensor.transpose(flat[:, P * i:P * (i + 1)],
                                               s_sub[t % 2][:, P * i:P * (i + 1)], ident[:, :])
                last.then_inc(p_xposed, 1)

            def weigh_values(n, t, p):
                pe.wait_ge(pT_ready, n + 1)
                after(pe, xatt_ready, n)
                for i in range(HH):
                    for b in range(2):
                        last = nc.tensor.matmul(
                            bank(7)[b * S:(b + 1) * S, 2 * HV * i:2 * HV * (i + 1)],
                            pT[t % 2][:, P * i + b * S:P * i + (b + 1) * S],
                            v2[p][:, 2 * t + b, i, :, :].rearrange("p h e -> p (h e)"),
                            start=True, stop=True)
                last.then_inc(pv_done, 1)

            def project_qk(src, w, dst, done):
                for half in range(2):
                    for b in range(2):
                        last = nc.tensor.matmul(
                            dst[b * S:(b + 1) * S, TG * S * half:TG * S * (half + 1)],
                            w[:, FH * half:FH * (half + 1)],
                            src[:, :].rearrange("p (t b k) -> p t b k", b=2, k=S)[:, :, b, :],
                            start=True, stop=True)
                last.then_inc(done, 1)

            def project_v():
                for u in range(2 * TG):
                    for h in range(2):
                        last = nc.tensor.matmul(bank(4)[h * S:(h + 1) * S, FH * u:FH * (u + 1)],
                                                cT[:, S * u:S * (u + 1)],
                                                w_xv[:, FH * h:FH * (h + 1)],
                                                start=True, stop=True)
                last.then_inc(xv_done, 1)

            def moe(g, t):
                nc.tensor.matmul(bank([4, 5, 6, 4][t])[:, 0:2 * D + NE], y2T[:, P * t:P * (t + 1)],
                                 w_moe[:, :], start=True, stop=True).then_inc(moe_done, 1)

            def phase3(s, p, slots=range(TG)):
                g, q, r = s + 1, 1 - p, s - 1
                for t in slots:
                    if t == 0 and exists(g):
                        after(pe, moe_ready, s * TG - TG - 2)
                        after(pe, klow_ready, g)
                        pe.wait_ge(ctx_loaded[q], (g - q) * 8 + 16)
                        transposes(ctx_in[q], bank(5), c_xposed)
                    if t < TG - 1 and exists(s):
                        scores(s * TG + t + 1, t + 1, p)
                    if t == TG - 1 and exists(g):
                        pe.wait_ge(kexp_ready, g + 1)
                        pe.wait_ge(kexp_loaded[q], (g - q) * (KDMA // 2) + KDMA)
                        pe.wait_ge(qlow_ready, g + 1)
                        scores(g * TG, 0, q)
                    if t == 0 and exists(g):
                        after(pe, moe_ready, s * TG - TG)
                        after(pe, v2_ready, g)
                        pe.wait_ge(y_copied, g + 1)
                        transposes(y_in[q], bank(4), y_xposed)
                    if exists(s):
                        turn_probabilities(s * TG + t, t)
                    if t == 1 and exists(r):
                        pe.wait_ge(xattT_ready, r + 1)
                        for u in range(TG):
                            last = nc.tensor.matmul(bank(6)[:, P * u:P * (u + 1)],
                                                    attT[:, P * u:P * (u + 1)], w_xo[:, :],
                                                    start=True, stop=True)
                        last.then_inc(xproj_done, 1)
                    if t == 2 and exists(g):
                        pe.wait_ge(qlow_ready, g + 1)
                        project_v()
                    if t == 3 and exists(r):
                        pe.wait_ge(y2T_ready, r + 1)
                        if exists(g):
                            pe.wait_ge(v2_ready, g + 1)
                            pe.wait_ge(klow_ready, g + 1)
                        moe(r, 0)
                        moe(r, 1)
                    if t == 0 and exists(g):
                        pe.wait_ge(cT_ready, g + 1)
                        project_qk(cT, w_xk, bank(5), xk_done)
                    if t == 0 and exists(r):
                        pe.wait_ge(xatt_ready, r * TG + TG)
                        after(pe, moe_ready, s * TG - TG)
                        transposes(att[q], bank(6), xatt_xposed)
                    if t == 1 and exists(g):
                        pe.wait_ge(yT_ready, g + 1)
                        project_qk(yT, w_xq, bank(4), xq_done)
                    if exists(s):
                        if t == 0:
                            pe.wait_ge(v2_ready, s + 1)
                        weigh_values(s * TG + t, t, p)
                    if t == 2 and exists(r):
                        pe.wait_ge(ln_b.done, r + 1)
                        transposes(y2, bank(6), y2_xposed)
                    if t == 3 and exists(r):
                        moe(r, 2)
                        pe.wait_ge(moe_ready, r * TG + 1)
                        moe(r, 3)

            pipeline(pe, phase1, last=NG - 2)
            phase2(-1, 1)
            phase1(NG - 1, 1)
            pe.wait_ge(w_loaded, ALL_WEIGHTS)
            pe.wait_ge(kvm_ready, NG * TG)
            pe.wait_ge(h2T_ready, 1)
            up(0, 0, 0)
            up(0, 0, 1)
            phase1(NG, 0)
            pe.wait_ge(att_ready, 2 * NG)
            phase2(0, 0, blocks=(2, 3))
            pipeline(pe, phase2, first=1, last=NG - 1)
            pe.wait_ge(rnd_ready, NF * NG)
            pe.wait_ge(const_ready, 3)
            pe.wait_ge(const_dve, 3)
            phase3(-1, 1, slots=(0, 1))
            phase2(NG, 0)
            phase3(-1, 1, slots=range(2, TG))
            pe.wait_ge(ysum_ready, NG)
            pipeline(pe, phase3, first=0, last=NG)


_ORDER = ["x", "ctx_1024", "mask_BxS2_ik0", "L0_attn_ln1_g", "L0_attn_ln1_b", "L0_attn_wq",
          "L0_attn_wk", "L0_attn_wv", "L0_attn_wo", "L0_attn_ln2_g", "L0_attn_ln2_b",
          "L0_attn_w1", "L0_attn_w2", "L0_xattn_WQ", "L0_xattn_WK", "L0_xattn_WV", "L0_xattn_WO",
          "L0_ffn_W_shared", "L0_ffn_W_expert", "L0_ffn_W_gate", "L0_ffn_bias"]


def kernel(**inputs):
    import concourse.bacc as bacc
    from concourse.bass_utils import run_bass_kernel_spmd

    a = {n: np.asarray(inputs[n]) for n in _ORDER}
    tokens, width = a["x"].shape[0] * a["x"].shape[1], a["x"].shape[2]
    a["x"] = a["x"].reshape(tokens, width)
    a["ctx_1024"] = a["ctx_1024"].reshape(tokens, width)
    a["mask_BxS2_ik0"] = a["mask_BxS2_ik0"].reshape(tokens // P, P).T
    for n in ("L0_attn_ln1_g", "L0_attn_ln1_b", "L0_attn_ln2_g", "L0_attn_ln2_b"):
        a[n] = a[n].reshape(width, 1)
    for n in ("L0_ffn_W_shared", "L0_ffn_W_expert"):
        a[n] = a[n].T
    a["L0_xattn_WV"] = a["L0_xattn_WV"].reshape(width, H // 2, 2, DH).transpose(0, 2, 1, 3) \
        .reshape(width, width)
    nc = bacc.Bacc("TRN2", target_bir_lowering=False, num_devices=1)
    arrays, args = {}, []
    for n in _ORDER:
        v = np.ascontiguousarray(a[n])
        arrays[f"in_{n}"] = v
        args.append(nc.dram_tensor(f"in_{n}", v.shape, mybir.dt.from_np(v.dtype),
                                   kind="ExternalInput").ap())
    args.append(nc.dram_tensor("out_rows", (tokens, width), F32, kind="ExternalOutput").ap())
    decoder_layer(nc, *args)
    r = run_bass_kernel_spmd(nc, [arrays], core_ids=[0])
    return r.results[0]["out_rows"].reshape(inputs["x"].shape)
```
